# Optimizing a Trainium2 kernel written in Bass

```python
import numpy as np
import jax
import jax.numpy as jnp

def _softmax(x, axis=-1):
    return jax.nn.softmax(x, axis=axis)

def _gelu(x):
    return jax.nn.gelu(x, approximate=True)

def _silu(x):
    return jax.nn.silu(x)

def _sigmoid(x):
    return jax.nn.sigmoid(x)

def _layernorm(x, axis=-1, eps=1e-05):
    m = jnp.mean(x, axis=axis, keepdims=True)
    v = jnp.var(x, axis=axis, keepdims=True)
    return (x - m) / jnp.sqrt(v + eps)

def _scatter_add(tgt, idx, src, axis=0):
    return tgt.at[idx].add(src)

def _segment_sum(src, seg, n):
    return jax.ops.segment_sum(src, seg, n)
kernel_name = 'mk_seq_preln_d1_jaxref_r8_7dae99'

def setup_inputs(seed: int=0):
    np.random.seed(seed)
    _w = jnp.asarray

    def _L0_attn_setup():
        import jax, jax.numpy as jnp
        import numpy as np
        import math
        DIM_EMB = 128
        DIM_QK = 128
        DIM_V = 128
        NORM_FACT = 1.0 / math.sqrt(DIM_EMB)
        key = jax.random.key(seed)
        k0, k1, k2, k3 = jax.random.split(key, 4)
        x = jax.random.normal(k0, (4, 512, DIM_EMB), dtype=jnp.float32)
        s = 1.0 / math.sqrt(DIM_EMB)
        Wq = jax.random.uniform(k1, (DIM_QK, DIM_EMB), jnp.float32, -s, s)
        Wk = jax.random.uniform(k2, (DIM_QK, DIM_EMB), jnp.float32, -s, s)
        Wv = jax.random.uniform(k3, (DIM_V, DIM_EMB), jnp.float32, -s, s)
        return {'x': x, 'Wq': Wq, 'Wk': Wk, 'Wv': Wv}
    _L0_attn_in = _L0_attn_setup()

    def _L0_ffn_setup():
        import jax, jax.numpy as jnp
        import numpy as np
        B, S, D, E = (4, 256, 128, 8)
        H = 2 * D
        key = jax.random.key(seed)
        ks = jax.random.split(key, 7)
        s_d = 1.0 / np.sqrt(D)
        s_h = 1.0 / np.sqrt(H)
        return {'x': jax.random.normal(ks[0], (B, S, D), dtype=jnp.float32), 'w_router': jax.random.normal(ks[1], (D, E), dtype=jnp.float32) * s_d, 'b_router': jnp.zeros((E,), dtype=jnp.float32), 'w1': jax.random.normal(ks[2], (E, D, H), dtype=jnp.float32) * s_d, 'b1': jnp.zeros((E, H), dtype=jnp.float32), 'w2': jax.random.normal(ks[3], (E, H, D), dtype=jnp.float32) * s_h, 'b2': jnp.zeros((E, D), dtype=jnp.float32)}
    _L0_ffn_in = _L0_ffn_setup()
    _d = {'L0_attn_x': _L0_attn_in['x'], 'L0_attn_Wq': _L0_attn_in['Wq'], 'L0_attn_Wk': _L0_attn_in['Wk'], 'L0_attn_Wv': _L0_attn_in['Wv'], 'L0_ffn_w_router': _L0_ffn_in['w_router'], 'L0_ffn_b_router': _L0_ffn_in['b_router'], 'L0_ffn_w1': _L0_ffn_in['w1'], 'L0_ffn_b1': _L0_ffn_in['b1'], 'L0_ffn_w2': _L0_ffn_in['w2'], 'L0_ffn_b2': _L0_ffn_in['b2']}
    _x0 = _d['L0_attn_x']
    _d['L0_attn_x'] = jax.random.normal(jax.random.fold_in(jax.random.key(seed), 1), (4, 1024, 128), dtype=_x0.dtype)
    del _x0
    return _d

def reference(L0_attn_x, L0_attn_Wq, L0_attn_Wk, L0_attn_Wv, L0_ffn_w_router, L0_ffn_b_router, L0_ffn_w1, L0_ffn_b1, L0_ffn_w2, L0_ffn_b2):

    def _L0_attn_ref(x, Wq, Wk, Wv):
        import jax, jax.numpy as jnp
        import numpy as np
        import math
        DIM_EMB = 128
        DIM_QK = 128
        DIM_V = 128
        NORM_FACT = 1.0 / math.sqrt(DIM_EMB)
        q = jnp.einsum('bne,de->bnd', x, Wq)
        k = jnp.einsum('bne,de->bnd', x, Wk)
        v = jnp.einsum('bne,de->bnd', x, Wv)
        logits = jnp.einsum('bnd,bmd->bnm', q, k)
        score = jax.nn.softmax(logits, axis=-1) * NORM_FACT
        att = jnp.einsum('bnm,bmv->bnv', score, v)
        return att

    def _L0_ffn_ref(x, w_router, b_router, w1, b1, w2, b2):
        import jax, jax.numpy as jnp
        import numpy as np
        B, S, D, E = (4, 256, 128, 8)
        H = 2 * D
        scores = jax.nn.softmax(x @ w_router + b_router, axis=2)
        expert_probs = jnp.max(scores, axis=2)
        expert_idx = jnp.argmax(scores, axis=2)
        h = jax.nn.relu(jnp.einsum('bsd,edh->ebsh', x, w1) + b1[:, None, None, :])
        y = jnp.einsum('ebsh,ehd->ebsd', h, w2) + b2[:, None, None, :]
        onehot = jax.nn.one_hot(expert_idx, E, dtype=x.dtype)
        out = jnp.einsum('ebsd,bse->bsd', y, onehot)
        return out * expert_probs[..., None]
    x = L0_attn_x
    x = x + _L0_attn_ref(_layernorm(x, axis=-1), L0_attn_Wq, L0_attn_Wk, L0_attn_Wv)
    x = x + _L0_ffn_ref(_layernorm(x, axis=-1), L0_ffn_w_router, L0_ffn_b_router, L0_ffn_w1, L0_ffn_b1, L0_ffn_w2, L0_ffn_b2)
    return x

_drawn_inputs = setup_inputs


def setup_inputs(seed=0):
    import zlib

    import numpy as np

    out = dict(_drawn_inputs(seed))
    spreads = {'L0_ffn_b_router': (0.0, 0.1), 'L0_ffn_b1': (0.0, 0.305), 'L0_ffn_b2': (0.0, 0.1)}
    factors = {}
    for name, (base, spread) in spreads.items():
        noise = np.random.default_rng([zlib.crc32(name.encode()), seed]).standard_normal(out[name].shape)
        drawn = base * np.exp(spread * noise) if base else spread * noise
        out[name] = jnp.asarray(drawn.astype(out[name].dtype))
    for name, factor in factors.items():
        out[name] = (out[name] * factor).astype(out[name].dtype)
    return out
```

```python
from contextlib import ExitStack

import concourse.bass as bass
from concourse import mybir

F32 = mybir.dt.float32
F32R = mybir.dt.float32r
BF16 = mybir.dt.bfloat16
I32 = mybir.dt.int32
ACT = mybir.ActivationFunctionType
ALU = mybir.AluOpType
AX = mybir.AxisListType

P = 128
EPS = 1e-5
ROUTE_STEPS = 27


def build_layer(nc, x, Wq, Wk, Wv, w_router, b_router, w1, b1, w2, b2, out):
    B, N, D = x.shape
    E, _, H = w1.shape
    T = 4
    G = T * P
    GROUPS = B * N // G
    PER_BATCH = N // G
    KC = N // P
    HC = H // P
    NORM = float(D) ** -0.5
    BLOCKS = (B * N - E) // P + E
    ROW = 2 * D + 4
    C_PROB, C_TOKEN, C_EXPERT = 2 * D, 2 * D + 1, 2 * D + 2
    NO_TOKEN = 1 << 20
    RING = 4
    BLOCKS_PEELED = 2 * RING - 1
    assert (BLOCKS - BLOCKS_PEELED) % RING == 0
    assert D == P and PER_BATCH == 2 and KC == 2 * T

    x_rows = x.rearrange("b n d -> (b n) d")
    x_tiles = x_rows.rearrange("(t p) d -> p t d", p=P)
    out_rows = out.rearrange("b n d -> (b n) d")
    table = nc.dram_tensor("expert_rows", (BLOCKS * P, ROW), F32, kind="Internal").ap()
    table_blocks = table.rearrange("(n p) c -> n p c", p=P)

    with ExitStack() as ctx:
        def sb(name, shape, dt=F32):
            return ctx.enter_context(nc.sbuf_tensor(name, shape, dt))

        def sem(name):
            return ctx.enter_context(nc.semaphore(name))

        x_all = sb("x_all", [P, GROUPS * T, D])
        keysT = sb("keysT", [P, 2, B * N], F32R)
        rows_hl = sb("rows_hl", [P, 2, GROUPS * T, D], F32R)
        values = sb("values", [P, 2, KC, D], F32R)
        probs = sb("probs", [P, 2 * T * N])
        qT = sb("qT", [P, 2, 2, G], F32R)
        probsT = sb("probsT", [P, 2, 2, G], F32R)
        xn = sb("xn", [P, 2, T, D])
        mixedT = sb("mixedT", [P, 2, G])
        pay = sb("pay", [P, 2, T, ROW])
        pay_i = pay[:, :, :, :].bitcast(I32)
        xn2T = sb("xn2T", [P, G])
        w1_sb = sb("w1_sb", [P, E, H])
        w2_sb = sb("w2_sb", [P, E, HC, D])
        b1_rep = sb("b1_rep", [P, E, H])
        b2_rep = sb("b2_rep", [P, E, D])
        wq_sb = sb("wq_sb", [P, D])
        wk_sb = sb("wk_sb", [P, D])
        wv_sb = sb("wv_sb", [P, D])
        wvT = sb("wvT", [P, D])
        m_hl = sb("m_hl", [P, 2, D], F32R)
        wr_sb = sb("wr_sb", [P, E])
        br_rep = sb("br_rep", [P, E])
        ident = sb("ident", [P, P])
        before_f = sb("before_f", [P, P])
        before = sb("before", [P, P], BF16)
        ones = sb("ones", [P, P], BF16)
        descend = sb("descend", [P, E])
        steps128 = sb("steps128", [P, T, E])
        tokens = sb("tokens", [P, GROUPS * T], I32)
        pad_rows = sb("pad_rows", [P, ROW])
        row_sum = sb("row_sum", [P, 2, T])
        weight = sb("weight", [P, 2, T])
        neg_max = sb("neg_max", [P, 2, T])
        stats1 = sb("stats1", [P, T, 6])
        mv1 = sb("mv1", [P, T, 2])
        rstd1 = sb("rstd1", [P, T])
        shift1 = sb("shift1", [P, T])
        stats2 = sb("stats2", [P, T, 6])
        mv2 = sb("mv2", [P, T, 2])
        newton = sb("newton", [P, 3, T])
        minus_half = sb("minus_half", [P, T])
        rstd2 = sb("rstd2", [P, T])
        shift2 = sb("shift2", [P, T])
        logit = sb("logit", [P, T, E])
        logit_max = sb("logit_max", [P, T])
        below = sb("below", [P, T, E])
        rank_key = sb("rank_key", [P, T, E])
        best_key = sb("best_key", [P, T])
        exps = sb("exps", [P, T, E])
        exp_sum = sb("exp_sum", [P, T])
        chosen = sb("chosen", [P, 2, T, E])
        chosen_b = sb("chosen_b", [P, T, E], BF16)
        counts = sb("counts", [P, T + 1, E])
        cap = sb("cap", [P, E])
        nxt = sb("nxt", [P, E])
        need = sb("need", [P, E])
        over = sb("over", [P, T, E])
        over2 = sb("over2", [P, 2, E])
        scan = sb("scan", [P, 4, 2 * E])
        fresh = sb("fresh", [P, E])
        delta = sb("delta", [P, E])
        moved = sb("moved", [P, E])
        room = sb("room", [P, E])
        place = sb("place", [P, T, E])
        place4 = sb("place4", [P, T, 4])
        place2 = sb("place2", [P, T, 2])
        place1 = sb("place1", [P, T])
        position = sb("position", [P, 2, T], I32)

        def probs_tile(parity, j):
            at = (parity * T + j) * N
            return probs[:, at:at + N]

        at = [0]

        def carve(n):
            at[0] += n
            return probs[:, at[0] - n:at[0]]

        block_in = [carve(ROW) for _ in range(RING)]
        block_T = [carve(P) for _ in range(2)]
        hidden = [carve(H) for _ in range(2)]
        hiddenT = [carve(H) for _ in range(2)]
        block_y = [carve(D) for _ in range(2)]
        block_out = [carve(D) for _ in range(RING)]

        ps_s = [ctx.enter_context(nc.psum_tensor(f"ps_s{n}", [P, N], F32)) for n in range(2)]
        ps_t = [ctx.enter_context(nc.psum_tensor(f"ps_t{n}", [P, G], F32)) for n in range(2)]
        ps_u = ctx.enter_context(nc.psum_tensor("ps_u", [P, G], F32))
        ps_m = ctx.enter_context(nc.psum_tensor("ps_m", [P, G], F32))

        x_in = [sem(f"x_in{n}") for n in range(3)]
        qk_in = sem("qk_in")
        v_in = sem("v_in")
        router_in = sem("router_in")
        experts_in = sem("experts_in")
        consts = sem("consts")
        passed = sem("passed")
        pads_ready = sem("pads_ready")
        ident_ready = sem("ident_ready")
        m_psum = sem("m_psum")
        m_hi = sem("m_hi")
        m_lo = sem("m_lo")
        wvT_psum = sem("wvT_psum")
        wvT_ready = sem("wvT_ready")
        ln1 = sem("ln1")
        scale1 = sem("scale1")
        xn_ready = sem("xn_ready")
        xT_psum = sem("xT_psum")
        xT_hi = sem("xT_hi")
        xT_lo = sem("xT_lo")
        q_psum = sem("q_psum")
        q_hi = sem("q_hi")
        q_lo = sem("q_lo")
        rows_hi = sem("rows_hi")
        rows_lo = sem("rows_lo")
        values_in = [sem(f"values_in{n}") for n in range(2)]
        s_psum = sem("s_psum")
        max_ready = sem("max_ready")
        exp_ready = sem("exp_ready")
        weight_ready = sem("weight_ready")
        pT_psum = sem("pT_psum")
        pT_hi = sem("pT_hi")
        pT_lo = sem("pT_lo")
        mixed = sem("mixed")
        mixedT_ready = sem("mixedT_ready")
        att_psum = sem("att_psum")
        x1_ready = sem("x1_ready")
        ln2 = sem("ln2")
        xn2_ready = sem("xn2_ready")
        xn2T_psum = sem("xn2T_psum")
        xn2T_ready = sem("xn2T_ready")
        logit_psum = sem("logit_psum")
        pick = sem("pick")
        exps_ready = sem("exps_ready")
        prob_ready = sem("prob_ready")
        chosen_ready = sem("chosen_ready")
        counts_psum = sem("counts_psum")
        counts_ready = sem("counts_ready")
        numbered = sem("numbered")
        route = sem("route")
        rows_out = [sem(f"rows_out{n}") for n in range(2)]
        b_in = [sem(f"b_in{n}") for n in range(RING)]
        b_x_psum = sem("b_x_psum")
        b_xT = sem("b_xT")
        b_up = sem("b_up")
        b_hidden = sem("b_hidden")
        b_t_psum = sem("b_t_psum")
        b_relu = sem("b_relu")
        b_down = sem("b_down")
        b_biased = sem("b_biased")
        b_done = sem("b_done")
        b_out = [sem(f"b_out{n}") for n in range(RING)]

        def wait(eng, s, value):
            if not isinstance(value, int) or value > 0:
                eng.wait_ge(s, value)

        def apart(eng):
            eng.sem_inc(passed, 1)

        def parts(s, b):
            found = [2 * b + s + d for d in (0, -1, -2, 2)]
            return [v if not isinstance(v, int) or 0 <= v < GROUPS else None for v in found]

        LAST = GROUPS + 2
        LOOP_FROM, LOOP_TO = 1, (GROUPS - 2) // 2

        def pipeline(eng, step):
            for i in range(2 * LOOP_FROM):
                step(i % 2, i // 2)
            with eng.Fori(LOOP_FROM, LOOP_TO) as b:
                for s in range(2):
                    step(s, b)
            for i in range(2 * LOOP_TO, LAST):
                step(i % 2, i // 2)

        LN1_STEPS = 2 * T
        LN2_STEPS = 2 * T + 13
        PICK_STEPS = 6
        CONSTS = 5 + E + T + 1 + 3 + 1

        ps_in = lambda a: (ps_u, ps_m)[a % 2][:, 0:P]
        ps_up = lambda a: ps_s[a % 2][:, 0:H]
        ps_hidden = lambda a: ps_s[a % 2][:, G:G + H]
        ps_down = lambda a: ps_t[a % 2][:, 0:D]

        def number(a, n):
            return a + RING * n

        def uses(a, n):
            return a // RING + n

        def load_expert(eng, a):
            cell = block_in[a % RING][0:1, C_EXPERT:C_EXPERT + 1].bitcast(I32)
            return eng.value_load(cell, min_val=0, max_val=E - 1)

        def blocks(eng, step):
            for a in range(BLOCKS_PEELED):
                step(a, 0)
            with eng.Fori(0, (BLOCKS - BLOCKS_PEELED) // RING) as n:
                for a in range(BLOCKS_PEELED, BLOCKS_PEELED + RING):
                    step(a, n)

        block = ctx.enter_context(nc.Block())

        @block.sync
        def _(sp):
            sp.dma_start(x_all[:, 0:T, :], x_tiles[:, 0:T, :]).then_inc(x_in[0], 16)
            sp.dma_start(wq_sb[:, :], Wq).then_inc(qk_in, 16)
            sp.dma_start(wk_sb[:, :], Wk).then_inc(qk_in, 16)
            sp.dma_start(x_all[:, T:2 * T, :], x_tiles[:, T:2 * T, :]).then_inc(x_in[1], 16)
            sp.dma_start(wv_sb[:, :], Wv).then_inc(v_in, 16)
            sp.dma_start(wr_sb[:, :], w_router).then_inc(router_in, 16)
            sp.dma_start(br_rep[:, :], b_router.partition_broadcast(P)).then_inc(router_in, 16)
            sp.dma_start(x_all[:, 2 * T:, :], x_tiles[:, 2 * T:, :]).then_inc(x_in[2], 16)

            def load_values(b):
                for h in range(2):
                    sp.wait_ge(rows_lo, 2 * b + h + 1)
                    apart(sp)
                    wait(sp, mixed, KC * (2 * b - 1) + T * h + T)
                    apart(sp)
                    sp.dma_start(values[:, :, T * h:T * h + T, :].bitcast(F32),
                                 rows_hl[:, :, bass.ds(b * KC + T * h, T), :].bitcast(F32)).then_inc(values_in[h], 16)

            load_values(0)
            sp.dma_start(w1_sb[:, :, :], w1.rearrange("e d h -> d e h")).then_inc(experts_in, 16)
            for c in range(HC):
                sp.dma_start(w2_sb[:, :, c, :], w2[:, c * P:(c + 1) * P, :].rearrange("e p d -> p e d"))\
                  .then_inc(experts_in, 16)
            sp.dma_start(b1_rep[:, :, :], b1.partition_broadcast(P)).then_inc(experts_in, 16)
            sp.dma_start(b2_rep[:, :, :], b2.partition_broadcast(P)).then_inc(experts_in, 16)
            with sp.Fori(1, B) as b:
                load_values(b)

            for n in range(2):
                sp.wait_ge(rows_out[n], 16 + 16 * T * GROUPS // 2)
            sp.wait_ge(pT_psum, KC * GROUPS)

            def load_block(a, n):
                wait(sp, b_out[a % RING], 16 * uses(a, n))
                apart(sp)
                rows = table_blocks[bass.ds(number(a, n), 1), :, :].rearrange("n p c -> p (n c)")
                sp.dma_start(block_in[a % RING], rows).then_inc(b_in[a % RING], 16)

            blocks(sp, load_block)
            for n in range(RING):
                sp.wait_ge(b_out[n], 16 * len(range(n, BLOCKS, RING)))

        @block.gpsimd
        def _(pool):
            pool.memset(ident[:, :], 0.0).then_inc(ident_ready, 1)
            pool.wait_ge(ident_ready, 1)
            pool.affine_select(out=ident[:, :], in_=ident[:, :], compare_op=ALU.not_equal, fill=1.0,
                               base=0, pattern=[[-1, P]], channel_multiplier=1).then_inc(ident_ready, 1)
            pool.memset(pad_rows[:, :], 0.0).then_inc(pads_ready, 1)
            pool.wait_ge(pads_ready, 1)
            pool.memset(pad_rows[:, C_TOKEN:C_TOKEN + 1].bitcast(I32), NO_TOKEN).then_inc(pads_ready, 1)
            pool.wait_ge(pads_ready, 2)
            table_columns = table.rearrange("(n p) c -> p n c", p=P)
            for n, (lo, hi) in enumerate(((0, BLOCKS // 2), (BLOCKS // 2, BLOCKS))):
                pool.dma_start(table_columns[:, lo:hi, :],
                             pad_rows[:, :].unsqueeze(1).to_broadcast([P, hi - lo, ROW])).then_inc(rows_out[n], 16)
            pool.memset(before_f[:, :], 1.0).then_inc(consts, 1)
            pool.wait_ge(consts, 1)
            pool.affine_select(out=before_f[:, :], in_=before_f[:, :], compare_op=ALU.is_gt, fill=0.0,
                               base=0, pattern=[[1, P]], channel_multiplier=-1).then_inc(consts, 1)
            pool.wait_ge(consts, 2)
            pool.tensor_copy(before[:, :], before_f[:, :]).then_inc(consts, 1)
            pool.memset(ones[:, :], 1.0).then_inc(consts, 1)
            pool.memset(minus_half[:, :], -0.5).then_inc(consts, 1)
            for e in range(E):
                pool.memset(descend[:, e:e + 1], float(E - e)).then_inc(consts, 1)
            for j in range(T):
                pool.memset(steps128[:, j, :], float(P * j)).then_inc(consts, 1)
            pool.iota(tokens[:, :], pattern=[[P, GROUPS * T]], base=0, channel_multiplier=1).then_inc(consts, 1)
            for state in (cap, nxt, scan):
                pool.memset(state[:], 0.0).then_inc(consts, 1)
            pool.memset(pay[:, :, :, ROW - 1:ROW], 0.0).then_inc(consts, 1)
            pool.wait_ge(consts, CONSTS)

            def scale_rows(k):
                pool.wait_ge(ln1, LN1_STEPS * k + LN1_STEPS)
                wait(pool, xn_ready, T * k)
                apart(pool)
                pool.tensor_scalar(rstd1[:, :], mv1[:, :, 1], EPS, None, ALU.add).then_inc(scale1, 1)
                pool.wait_ge(scale1, 4 * k + 1)
                pool.tensor_tensor(rstd1[:, :], rstd1[:, :], minus_half[:, :], ALU.pow).then_inc(scale1, 1)
                pool.wait_ge(scale1, 4 * k + 2)
                pool.tensor_tensor(shift1[:, :], mv1[:, :, 0], rstd1[:, :], ALU.mult).then_inc(scale1, 1)
                pool.wait_ge(scale1, 4 * k + 3)
                apart(pool)
                pool.tensor_scalar(shift1[:, :], shift1[:, :], -1.0, None, ALU.mult).then_inc(scale1, 1)

            def split_rows(k, s):
                pool.wait_ge(rows_hi, k + 1)
                tiles = bass.ds(k * T, T)
                pool.tensor_tensor(rows_hl[:, 1, tiles, :], xn[:, s, :, :],
                                   rows_hl[:, 0, tiles, :].bitcast(F32), ALU.subtract).then_inc(rows_lo, 1)

            def number_rows(r, s, b):
                wait(pool, rows_out[s], 16 + (b - 1) * 16 * T)
                apart(pool)
                pool.tensor_copy(pay_i[:, s, :, C_TOKEN], tokens[:, bass.ds(r * T, T)]).then_inc(numbered, 1)
                pool.wait_ge(pick, PICK_STEPS * r + 5)
                apart(pool)
                pool.tensor_scalar(pay_i[:, s, :, C_EXPERT], best_key[:, :], -1.0, float(E),
                                   ALU.mult, ALU.add).then_inc(numbered, 1)

            def place_rows(r, s):
                done = [0]

                def then(ins, alone=False):
                    done[0] += 1
                    ins.then_inc(route, 1)
                    pool.wait_ge(route, r * ROUTE_STEPS + done[0])
                    if alone:
                        apart(pool)

                over_tiles = lambda v: v.unsqueeze(1).to_broadcast([P, T, E])
                tt = pool.tensor_tensor
                total = counts[:, T, :]
                ranks = counts[:, 0:T, :]
                pool.wait_ge(counts_ready, r + 1)
                pool.wait_ge(pick, PICK_STEPS * r + 6)
                then(tt(need[:, :], total, cap[:, :], ALU.subtract))
                then(tt(over[:, :, :], over_tiles(need[:, :]), steps128[:, :, :], ALU.subtract), alone=True)
                then(pool.tensor_scalar(over[:, :, :], over[:, :, :], 0.0, None, ALU.is_gt))
                then(tt(over2[:, :, :], over[:, 0:2, :], over[:, 2:4, :], ALU.add))
                then(tt(scan[:, 0, E:2 * E], over2[:, 0, :], over2[:, 1, :], ALU.add))
                for n in range(3):
                    then(tt(scan[:, n + 1, E - 1:2 * E], scan[:, n, E - 1:2 * E],
                            scan[:, n, E - 1 - (1 << n):2 * E - (1 << n)], ALU.add), alone=True)
                then(pool.tensor_scalar(fresh[:, :], scan[:, 3, E - 1:2 * E - 1], float(P), None, ALU.mult))
                then(tt(fresh[:, :], fresh[:, :], cap[:, :], ALU.subtract))
                then(tt(delta[:, :], fresh[:, :], nxt[:, :], ALU.subtract))
                then(tt(place[:, :, :], ranks, over_tiles(cap[:, :]), ALU.subtract), alone=True)
                then(pool.tensor_scalar(place[:, :, :], place[:, :, :], 0.0, None, ALU.is_ge))
                then(tt(place[:, :, :], place[:, :, :], over_tiles(delta[:, :]), ALU.mult))
                then(tt(place[:, :, :], place[:, :, :], ranks, ALU.add))
                then(tt(place[:, :, :], place[:, :, :], over_tiles(nxt[:, :]), ALU.add))
                then(tt(place[:, :, :], place[:, :, :], chosen[:, s, :, :], ALU.mult))
                then(tt(place4[:, :, :], place[:, :, 0:4], place[:, :, 4:8], ALU.add))
                then(tt(place2[:, :, :], place4[:, :, 0:2], place4[:, :, 2:4], ALU.add))
                then(tt(place1[:, :], place2[:, :, 0], place2[:, :, 1], ALU.add), alone=True)
                then(pool.tensor_copy(position[:, s, :], place1[:, :]))
                then(tt(moved[:, :], over[:, 0, :], delta[:, :], ALU.mult))
                then(tt(nxt[:, :], nxt[:, :], moved[:, :], ALU.add))
                then(tt(nxt[:, :], nxt[:, :], total, ALU.add), alone=True)
                then(pool.tensor_scalar(room[:, :], scan[:, 0, E:2 * E], float(P), None, ALU.mult))
                then(tt(cap[:, :], room[:, :], need[:, :], ALU.subtract))
                then(tt(scan[:, 0, E - 1:E], scan[:, 0, E - 1:E], scan[:, 3, 2 * E - 1:2 * E], ALU.add))
                assert done[0] == ROUTE_STEPS
                pool.wait_ge(numbered, 2 * r + 2)
                pool.wait_ge(xn2_ready, T * r + T)
                pool.wait_ge(x1_ready, T * r + T)
                pool.wait_ge(prob_ready, 2 * r + 2)
                apart(pool)
                for j in range(T):
                    pool.indirect_dma_start(
                        out=table[:, :], out_offset=bass.IndirectOffsetOnAxis(ap=position[:, s, j:j + 1], axis=0),
                        in_=pay[:, s, j, :], in_offset=None,
                        bounds_check=BLOCKS * P - 1, oob_is_err=False).then_inc(rows_out[s], 16)

            for k in range(2):
                scale_rows(k)
            for k in range(2):
                split_rows(k, k)
            for n in range(2):
                pool.wait_ge(rows_out[n], 16)

            def step(s, b):
                g, p, r, k = parts(s, b)
                if k is not None:
                    scale_rows(k)
                if r is not None:
                    number_rows(r, s, b)
                if k is not None:
                    split_rows(k, s)
                if r is not None:
                    place_rows(r, s)

            pipeline(pool, step)

            def scatter_block(a, n):
                pool.wait_ge(b_done, number(a, n) + 1)
                apart(pool)
                pool.indirect_dma_start(
                    out=out_rows, in_=block_out[a % RING], in_offset=None,
                    out_offset=bass.IndirectOffsetOnAxis(
                        ap=block_in[a % RING][:, C_TOKEN:C_TOKEN + 1].bitcast(I32), axis=0),
                    bounds_check=B * N - 1, oob_is_err=False).then_inc(b_out[a % RING], 16)

            blocks(pool, scatter_block)

        @block.vector
        def _(dve):
            tt = dve.tensor_tensor

            def stats(src, bn, mv, count, base, part):
                if part in (0, None):
                    for j in range(T):
                        dve.bn_stats(out=bn[:, j, :], in_=src(j)).then_inc(count, 1)
                if part in (1, None):
                    for j in range(T):
                        dve.wait_ge(count, base + j + 1)
                        apart(dve)
                        dve.bn_aggr(out=mv[:, j, :], in_=bn[:, j, :]).then_inc(count, 1)

            def stats1_of(k, s, part=None):
                if part in (0, None):
                    if isinstance(k, int) and k < 2:
                        dve.wait_ge(x_in[k], 16)
                    else:
                        dve.wait_ge(x_in[2], 16)
                    wait(dve, scale1, 4 * k)
                stats(lambda j: x_all[:, bass.ds(k * T + j, 1), :].rearrange("p a d -> p (a d)"),
                      stats1, mv1, ln1, LN1_STEPS * k, part)

            def xT_lo_of(k):
                dve.wait_ge(xT_hi, k + 1)
                cols = bass.ds(k * G, G)
                tt(keysT[:, 1, cols], ps_m[:, :], keysT[:, 0, cols].bitcast(F32), ALU.subtract).then_inc(xT_lo, 1)

            def q_lo_of(k, s):
                dve.wait_ge(q_hi, k + 1)
                tt(qT[:, s, 1, :], ps_m[:, :], qT[:, s, 0, :].bitcast(F32), ALU.subtract).then_inc(q_lo, 1)

            stats1_of(0, 0)
            dve.wait_ge(m_hi, 1)
            tt(m_hl[:, 1, :], ps_t[0][:, 0:D], m_hl[:, 0, :].bitcast(F32), ALU.subtract).then_inc(m_lo, 1)
            xT_lo_of(0)
            stats1_of(1, 1)
            q_lo_of(0, 0)
            xT_lo_of(1)
            q_lo_of(1, 1)
            dve.wait_ge(router_in, 32)
            dve.wait_ge(consts, CONSTS)

            def step(s, b):
                g, p, r, k = parts(s, b)
                q = 1 - s

                def row_max(j):
                    if g is None:
                        return
                    dve.wait_ge(s_psum, T * g + j + 1)
                    wait(dve, exp_ready, T * (g - 2) + j + 1)
                    dve.tensor_reduce(out=neg_max[:, s, j:j + 1], in_=ps_s[j % 2][:, :], axis=AX.X,
                                      op=ALU.max, negate=True).then_inc(max_ready, 1)

                def lo(c):
                    if p is None:
                        return
                    dve.wait_ge(pT_hi, KC * p + c + 1)
                    wait(dve, mixed, KC * p + c - 1)
                    tt(probsT[:, c % 2, 1, :], ps_t[c % 2][:, :], probsT[:, c % 2, 0, :].bitcast(F32),
                       ALU.subtract).then_inc(pT_lo, 1)

                def weights():
                    dve.wait_ge(exp_ready, T * p + T)
                    dve.reciprocal(weight[:, q, :], row_sum[:, q, :]).then_inc(weight_ready, 1)
                    dve.wait_ge(weight_ready, 2 * p + 1)
                    dve.tensor_scalar(weight[:, q, :], weight[:, q, :], NORM, None, ALU.mult)\
                       .then_inc(weight_ready, 1)

                def residual(j):
                    if j == 0:
                        dve.wait_ge(att_psum, r + 1)
                        dve.wait_ge(weight_ready, 2 * r + 2)
                        wait(dve, rows_out[s], 16 + (b - 1) * 16 * T)
                    dve.scalar_tensor_tensor(
                        pay[:, s, j, D:2 * D], ps_m[:, j * D:(j + 1) * D], weight[:, s, j:j + 1],
                        x_all[:, bass.ds(r * T + j, 1), :].rearrange("p a d -> p (a d)"),
                        ALU.mult, ALU.add).then_inc(x1_ready, 1)

                def stats2_of(part):
                    if part == 0:
                        dve.wait_ge(x1_ready, T * r + T)
                        wait(dve, xn2_ready, T * r)
                    stats(lambda j: pay[:, s, j, D:2 * D], stats2, mv2, ln2, LN2_STEPS * r, part)

                def scale2():
                    done = [2 * T]

                    def then(ins):
                        done[0] += 1
                        ins.then_inc(ln2, 1)
                        if done[0] < LN2_STEPS:
                            dve.wait_ge(ln2, LN2_STEPS * r + done[0])

                    bits = newton[:, 1, :].bitcast(I32)
                    dve.wait_ge(ln2, LN2_STEPS * r + 2 * T)
                    then(dve.tensor_scalar(newton[:, 0, :], mv2[:, :, 1], EPS, None, ALU.add))
                    then(dve.tensor_scalar(bits, newton[:, 0, :].bitcast(I32), 1, None, ALU.logical_shift_right))
                    then(dve.tensor_scalar(rstd2[:, :].bitcast(I32), bits, -1.0, float(0x5f3759df),
                                           ALU.mult, ALU.add))
                    for n in range(3):
                        then(tt(newton[:, 1, :], rstd2[:, :], rstd2[:, :], ALU.mult))
                        then(dve.scalar_tensor_tensor(newton[:, 2, :], newton[:, 1, :], -0.5, newton[:, 0, :],
                                                      ALU.mult, ALU.mult))
                        then(dve.scalar_tensor_tensor(rstd2[:, :], newton[:, 2, :], 1.5, rstd2[:, :],
                                                      ALU.add, ALU.mult))
                    then(dve.scalar_tensor_tensor(shift2[:, :], mv2[:, :, 0], -1.0, rstd2[:, :],
                                                  ALU.mult, ALU.mult))
                    assert done[0] == LN2_STEPS

                def choose():
                    per_expert = lambda v: v.unsqueeze(2).to_broadcast([P, T, E])
                    over_tiles = lambda v: v.unsqueeze(1).to_broadcast([P, T, E])
                    dve.wait_ge(logit_psum, r + 1)
                    tt(logit[:, :, :], ps_m[:, 0:T * E].rearrange("p (t e) -> p t e", e=E),
                       over_tiles(br_rep[:, :]), ALU.add).then_inc(pick, 1)
                    dve.wait_ge(pick, PICK_STEPS * r + 1)
                    dve.tensor_reduce(out=logit_max[:, :], in_=logit[:, :, :], axis=AX.X,
                                      op=ALU.max).then_inc(pick, 1)
                    dve.wait_ge(pick, PICK_STEPS * r + 2)
                    wait(dve, exps_ready, r)
                    tt(below[:, :, :], logit[:, :, :], per_expert(logit_max[:, :]), ALU.subtract)\
                        .then_inc(pick, 1)
                    dve.wait_ge(pick, PICK_STEPS * r + 3)
                    wait(dve, numbered, 2 * r)
                    dve.scalar_tensor_tensor(rank_key[:, :, :], below[:, :, :], 0.0, over_tiles(descend[:, :]),
                                             ALU.is_ge, ALU.mult).then_inc(pick, 1)
                    dve.wait_ge(pick, PICK_STEPS * r + 4)
                    dve.tensor_reduce(out=best_key[:, :], in_=rank_key[:, :, :], axis=AX.X,
                                      op=ALU.max).then_inc(pick, 1)
                    dve.wait_ge(pick, PICK_STEPS * r + 5)
                    wait(dve, counts_psum, r)
                    tt(chosen_b[:, :, :], rank_key[:, :, :], per_expert(best_key[:, :]), ALU.is_equal)\
                        .then_inc(chosen_ready, 1)
                    tt(chosen[:, s, :, :], rank_key[:, :, :], per_expert(best_key[:, :]), ALU.is_equal)\
                        .then_inc(pick, 1)

                def probability():
                    dve.wait_ge(exps_ready, r + 1)
                    dve.reduce_sum(exp_sum[:, :], exps[:, :, :], axis=AX.X).then_inc(prob_ready, 1)
                    dve.wait_ge(prob_ready, 2 * r + 1)
                    dve.reciprocal(pay[:, s, :, C_PROB], exp_sum[:, :]).then_inc(prob_ready, 1)

                row_max(0)
                if p is not None:
                    weights()
                lo(0)
                if r is not None:
                    residual(0)
                    residual(1)
                lo(1)
                if r is not None:
                    residual(2)
                    residual(3)
                lo(2)
                row_max(1)
                if r is not None:
                    stats2_of(0)
                lo(3)
                if r is not None:
                    stats2_of(1)
                    scale2()
                lo(4)
                row_max(2)
                if k is not None:
                    stats1_of(k, s, 0)
                lo(5)
                if k is not None:
                    stats1_of(k, s, 1)
                lo(6)
                row_max(3)
                if r is not None:
                    choose()
                lo(7)
                if k is not None:
                    xT_lo_of(k)
                if r is not None:
                    probability()
                if k is not None:
                    q_lo_of(k, s)

            pipeline(dve, step)

            dve.wait_ge(experts_in, 16 * (3 + HC))

            def hidden_of(a, n, expert):
                t = number(a, n)
                dve.wait_ge(b_up, t + 1)
                wait(dve, b_t_psum, t - 1)
                tt(hidden[a % 2], ps_up(a), b1_rep[:, bass.ds(expert, 1), :].rearrange("p a h -> p (a h)"),
                   ALU.add).then_inc(b_hidden, 1)

            def output_of(a, n, expert):
                t = number(a, n)
                rows = block_in[a % RING]
                dve.wait_ge(b_down, t + 1)
                tt(block_y[a % 2], ps_down(a), b2_rep[:, bass.ds(expert, 1), :].rearrange("p a d -> p (a d)"),
                   ALU.add).then_inc(b_biased, 1)
                dve.wait_ge(b_biased, t + 1)
                wait(dve, b_out[a % RING], 16 * uses(a, n))
                dve.scalar_tensor_tensor(block_out[a % RING], block_y[a % 2], rows[:, C_PROB:C_PROB + 1],
                                         rows[:, D:2 * D], ALU.mult, ALU.add).then_inc(b_done, 1)

            def block_step(a, n):
                dve.wait_ge(b_in[a % RING], 16 * (uses(a, n) + 1))
                apart(dve)
                hidden_of(a, n, load_expert(dve, a))
                if a > 0:
                    output_of(a - 1, n, load_expert(dve, a - 1))

            blocks(dve, block_step)
            last = BLOCKS - 1
            output_of(last, 0, load_expert(dve, last))

        @block.scalar
        def _(act):
            ln_apply = lambda dst, src, rstd, shift: act.activation(dst, src, ACT.Identity, bias=shift, scale=rstd)

            def norm1(k, s):
                act.wait_ge(scale1, 4 * k + 4)
                wait(act, xT_psum, k - 1)
                wait(act, rows_lo, k - 1)
                for j in range(T):
                    ln_apply(xn[:, s, j, :], x_all[:, bass.ds(k * T + j, 1), :].rearrange("p a d -> p (a d)"),
                             rstd1[:, j:j + 1], shift1[:, j:j + 1]).then_inc(xn_ready, 1)

            def rows_hi_of(k, s):
                act.wait_ge(xn_ready, T * k + T)
                act.copy(rows_hl[:, 0, bass.ds(k * T, T), :], xn[:, s, :, :]).then_inc(rows_hi, 1)

            def xT_hi_of(k):
                act.wait_ge(xT_psum, k + 1)
                act.copy(keysT[:, 0, bass.ds(k * G, G)], ps_m[:, :]).then_inc(xT_hi, 1)

            def q_hi_of(k, s):
                act.wait_ge(q_psum, k + 1)
                wait(act, s_psum, T * (k - 2) + T)
                act.copy(qT[:, s, 0, :], ps_m[:, :]).then_inc(q_hi, 1)

            act.wait_ge(m_psum, 1)
            act.copy(m_hl[:, 0, :], ps_t[0][:, 0:D]).then_inc(m_hi, 1)
            norm1(0, 0)
            xT_hi_of(0)
            rows_hi_of(0, 0)
            q_hi_of(0, 0)
            norm1(1, 1)
            xT_hi_of(1)
            rows_hi_of(1, 1)
            q_hi_of(1, 1)
            act.wait_ge(wvT_psum, 1)
            act.copy(wvT[:, :], ps_t[1][:, 0:D]).then_inc(wvT_ready, 1)

            def step(s, b):
                g, p, r, k = parts(s, b)
                q = 1 - s

                def exponentials(j):
                    if g is None:
                        return
                    act.wait_ge(max_ready, T * g + j + 1)
                    if j == 0:
                        wait(act, pT_psum, KC * (g - 2) + KC)
                        wait(act, weight_ready, 2 * (g - 2) + 2)
                    act.activation(probs_tile(s, j), ps_s[j % 2][:, :], ACT.Exp, bias=neg_max[:, s, j:j + 1],
                                   accum_out=row_sum[:, s, j:j + 1]).then_inc(exp_ready, 1)

                def hi(c):
                    if p is None:
                        return
                    act.wait_ge(pT_psum, KC * p + c + 1)
                    wait(act, mixed, KC * p + c - 1)
                    act.copy(probsT[:, c % 2, 0, :], ps_t[c % 2][:, :]).then_inc(pT_hi, 1)

                def norm2():
                    act.wait_ge(ln2, LN2_STEPS * r + LN2_STEPS)
                    wait(act, rows_out[s], 16 + (b - 1) * 16 * T)
                    for j in range(T):
                        ln_apply(pay[:, s, j, 0:D], pay[:, s, j, D:2 * D], rstd2[:, j:j + 1],
                                 shift2[:, j:j + 1]).then_inc(xn2_ready, 1)

                if r is not None:
                    act.wait_ge(mixed, KC * r + KC)
                    wait(act, att_psum, r)
                    act.copy(mixedT[:, s, :], ps_u[:, :]).then_inc(mixedT_ready, 1)
                hi(0)
                exponentials(0)
                hi(1)
                hi(2)
                exponentials(1)
                hi(3)
                if r is not None:
                    norm2()
                hi(4)
                exponentials(2)
                if r is not None:
                    act.wait_ge(xn2T_psum, r + 1)
                    wait(act, logit_psum, r)
                    act.copy(xn2T[:, :], ps_m[:, :]).then_inc(xn2T_ready, 1)
                hi(5)
                if k is not None:
                    norm1(k, s)
                hi(6)
                exponentials(3)
                if k is not None:
                    rows_hi_of(k, s)
                hi(7)
                if k is not None:
                    xT_hi_of(k)
                if r is not None:
                    act.wait_ge(pick, PICK_STEPS * r + 3)
                    wait(act, prob_ready, 2 * r)
                    act.activation(exps[:, :, :], below[:, :, :], ACT.Exp).then_inc(exps_ready, 1)
                if k is not None:
                    q_hi_of(k, s)
                if r is not None:
                    act.wait_ge(counts_psum, r + 1)
                    wait(act, route, ROUTE_STEPS * r)
                    act.copy(counts[:, :, :], ps_m[:, 0:(T + 1) * E].rearrange("p (t e) -> p t e", e=E))\
                       .then_inc(counts_ready, 1)

            pipeline(act, step)

            def transposed(a, n):
                t = number(a, n)
                act.wait_ge(b_x_psum, t + 1)
                wait(act, b_up, t - 1)
                act.copy(block_T[a % 2], ps_in(a)).then_inc(b_xT, 1)

            def relu(a, n):
                t = number(a, n)
                act.wait_ge(b_t_psum, t + 1)
                wait(act, b_down, t - 1)
                act.activation(hiddenT[a % 2], ps_hidden(a), ACT.Relu).then_inc(b_relu, 1)

            def block_step(a, n):
                transposed(a, n)
                if a > 0:
                    relu(a - 1, n)

            blocks(act, block_step)
            relu(BLOCKS - 1, 0)

        @block.tensor
        def _(pe):
            HI_LO = ((0, 0), (0, 1), (1, 0))

            def transpose_rows(k, s):
                pe.wait_ge(xn_ready, T * k + T)
                for j in range(T):
                    last = pe.transpose(ps_m[:, j * P:(j + 1) * P], xn[:, s, j, :], ident[:, :])
                last.then_inc(xT_psum, 1)

            def queries(k):
                pe.wait_ge(xT_lo, k + 1)
                for n, (wh, xh) in enumerate(HI_LO):
                    last = pe.matmul(ps_m[:, :], m_hl[:, wh, :], keysT[:, xh, bass.ds(k * G, G)],
                                     start=(n == 0), stop=(n == 2))
                last.then_inc(q_psum, 1)

            pe.wait_ge(qk_in, 32)
            pe.matmul(ps_t[0][:, 0:D], wq_sb[:, :], wk_sb[:, :], start=True, stop=True).then_inc(m_psum, 1)
            pe.wait_ge(ident_ready, 2)
            pe.wait_ge(v_in, 16)
            pe.transpose(ps_t[1][:, 0:D], wv_sb[:, :], ident[:, :]).then_inc(wvT_psum, 1)
            transpose_rows(0, 0)
            pe.wait_ge(m_lo, 1)
            queries(0)
            pe.wait_ge(q_lo, 1)
            transpose_rows(1, 1)
            queries(1)
            pe.wait_ge(wvT_ready, 1)
            pe.wait_ge(router_in, 32)
            pe.wait_ge(consts, CONSTS)

            def step(s, b):
                g, p, r, k = parts(s, b)
                q = 1 - s

                def logits(j):
                    if g is None:
                        return
                    if j == 0:
                        pe.wait_ge(q_lo, g + 1)
                        pe.wait_ge(xT_lo, PER_BATCH * (b + 1))
                    wait(pe, exp_ready, T * g + j - 1)
                    for n, (qh, kh) in enumerate(HI_LO):
                        for h in range(N // G):
                            last = pe.matmul(ps_s[j % 2][:, h * G:(h + 1) * G], qT[:, s, qh, j * P:(j + 1) * P],
                                             keysT[:, kh, bass.ds(b * N + h * G, G)],
                                             start=(n == 0), stop=(n == 2))
                    last.then_inc(s_psum, 1)

                def transposes(c):
                    if p is None:
                        return
                    if c == 0:
                        pe.wait_ge(exp_ready, T * p + T)
                    wait(pe, pT_lo, KC * p + c - 1)
                    for j in range(T):
                        last = pe.transpose(ps_t[c % 2][:, j * P:(j + 1) * P],
                                            probs_tile(q, j)[:, c * P:(c + 1) * P], ident[:, :])
                    last.then_inc(pT_psum, 1)

                def mix(c):
                    if p is None:
                        return
                    if c % T == 0:
                        pe.wait_ge(values_in[c // T], 16 * (b + 1 - q))
                    if c == 0:
                        wait(pe, mixedT_ready, p)
                    pe.wait_ge(pT_lo, KC * p + c + 1)
                    for n, (vh, ph) in enumerate(HI_LO):
                        last = pe.matmul(ps_u[:, :], values[:, vh, c, :], probsT[:, c % 2, ph, :],
                                         start=(c == 0 and n == 0), stop=(c == KC - 1 and n == 2))
                    last.then_inc(mixed, 1)

                def attend():
                    pe.wait_ge(mixedT_ready, r + 1)
                    wait(pe, counts_ready, r)
                    pe.wait_ge(q_lo, k if k is not None else GROUPS)
                    for j in range(T):
                        last = pe.matmul(ps_m[:, j * D:(j + 1) * D], mixedT[:, s, j * P:(j + 1) * P], wvT[:, :],
                                         start=True, stop=True)
                    last.then_inc(att_psum, 1)

                def transpose_xn2():
                    pe.wait_ge(xn2_ready, T * r + T)
                    pe.wait_ge(x1_ready, T * r + T)
                    for j in range(T):
                        last = pe.transpose(ps_m[:, j * P:(j + 1) * P], pay[:, s, j, 0:D], ident[:, :])
                    last.then_inc(xn2T_psum, 1)

                def router():
                    pe.wait_ge(xn2T_ready, r + 1)
                    for j in range(T):
                        last = pe.matmul(ps_m[:, j * E:(j + 1) * E], xn2T[:, j * P:(j + 1) * P], wr_sb[:, :],
                                         start=True, stop=True)
                    last.then_inc(logit_psum, 1)

                def count():
                    pe.wait_ge(chosen_ready, r + 1)
                    if k is not None:
                        pe.wait_ge(q_lo, k + 1)
                    for j in range(T + 1):
                        out_j = ps_m[:, j * E:(j + 1) * E]
                        for i in range(min(j, T)):
                            last = pe.matmul(out_j, ones[:, :], chosen_b[:, i, :], start=(i == 0),
                                             stop=(j == T and i == T - 1))
                        if j < T:
                            last = pe.matmul(out_j, before[:, :], chosen_b[:, j, :], start=(j == 0), stop=True)
                    last.then_inc(counts_psum, 1)

                if p is not None:
                    logits(0)
                    transposes(0)
                else:
                    logits(0)
                if r is not None:
                    attend()
                mix(0)
                transposes(1)
                transposes(2)
                logits(1)
                mix(1)
                mix(2)
                transposes(3)
                transposes(4)
                logits(2)
                mix(3)
                if r is not None:
                    transpose_xn2()
                mix(4)
                transposes(5)
                transposes(6)
                logits(3)
                mix(5)
                if r is not None:
                    router()
                mix(6)
                transposes(7)
                if k is not None:
                    if r is not None:
                        pe.wait_ge(pick, PICK_STEPS * r + 1)
                    else:
                        pe.wait_ge(q_lo, k)
                    transpose_rows(k, s)
                mix(7)
                if k is not None:
                    queries(k)
                if r is not None:
                    count()

            pipeline(pe, step)

            pe.wait_ge(experts_in, 16 * (3 + HC))
            pe.wait_ge(counts_ready, GROUPS)

            def transpose_block(a, n):
                pe.wait_ge(b_in[a % RING], 16 * (uses(a, n) + 1))
                wait(pe, b_xT, number(a, n) - 1)
                pe.transpose(ps_in(a), block_in[a % RING][:, 0:D], ident[:, :]).then_inc(b_x_psum, 1)

            def up(a, n, expert):
                t = number(a, n)
                pe.wait_ge(b_xT, t + 1)
                wait(pe, b_hidden, t - 1)
                pe.matmul(ps_up(a), block_T[a % 2], w1_sb[:, bass.ds(expert, 1), :].rearrange("p a h -> p (a h)"),
                          start=True, stop=True).then_inc(b_up, 1)

            def transpose_hidden(a, n):
                t = number(a, n)
                pe.wait_ge(b_hidden, t + 1)
                wait(pe, b_relu, t - 1)
                for c in range(HC):
                    last = pe.transpose(ps_hidden(a)[:, c * P:(c + 1) * P], hidden[a % 2][:, c * P:(c + 1) * P],
                                        ident[:, :])
                last.then_inc(b_t_psum, 1)

            def down(a, n, expert):
                t = number(a, n)
                pe.wait_ge(b_relu, t + 1)
                wait(pe, b_biased, t - 1)
                for c in range(HC):
                    last = pe.matmul(ps_down(a), hiddenT[a % 2][:, c * P:(c + 1) * P],
                                     w2_sb[:, bass.ds(expert, 1), c, :].rearrange("p a d -> p (a d)"),
                                     start=(c == 0), stop=(c == HC - 1))
                last.then_inc(b_down, 1)

            def block_step(a, n):
                transpose_block(a, n)
                if a > 1:
                    down(a - 2, n, load_expert(pe, a - 2))
                if a > 0:
                    transpose_hidden(a - 1, n)
                up(a, n, load_expert(pe, a))

            blocks(pe, block_step)
            last = BLOCKS - 1
            down(last - 1, 0, load_expert(pe, last - 1))
            transpose_hidden(last, 0)
            down(last, 0, load_expert(pe, last))


_INS = ['L0_attn_x', 'L0_attn_Wq', 'L0_attn_Wk', 'L0_attn_Wv', 'L0_ffn_w_router', 'L0_ffn_b_router',
        'L0_ffn_w1', 'L0_ffn_b1', 'L0_ffn_w2', 'L0_ffn_b2']


def kernel(**inputs):
    import numpy as _np
    import concourse.bacc as _bacc
    from concourse import mybir as _mybir
    from concourse.bass_utils import run_bass_kernel_spmd as _run

    nc = _bacc.Bacc("TRN2", target_bir_lowering=False, num_devices=1)
    arrays, args = {}, []
    for name in _INS:
        a = _np.ascontiguousarray(inputs[name])
        arrays[f"in_{name}"] = a
        args.append(nc.dram_tensor(f"in_{name}", a.shape, _mybir.dt.from_np(a.dtype), kind="ExternalInput").ap())
    shape = inputs['L0_attn_x'].shape
    out = nc.dram_tensor("out", shape, _mybir.dt.from_np(_np.dtype("float32")), kind="ExternalOutput").ap()
    build_layer(nc, *args, out)
    r = _run(nc, [arrays], core_ids=[0])
    return r.results[0]["out"]
```

```python
from contextlib import ExitStack

import concourse.bass as bass
from concourse import mybir

F32 = mybir.dt.float32
F32R = mybir.dt.float32r
BF16 = mybir.dt.bfloat16
I32 = mybir.dt.int32
ACT = mybir.ActivationFunctionType
ALU = mybir.AluOpType
AX = mybir.AxisListType

P = 128
EPS = 1e-5
ROUTE_STEPS = 27


def build_layer(nc, x, Wq, Wk, Wv, w_router, b_router, w1, b1, w2, b2, out):
    B, N, D = x.shape
    E, _, H = w1.shape
    T = 4
    G = T * P
    GROUPS = B * N // G
    PER_BATCH = N // G
    KC = N // P
    HC = H // P
    NORM = float(D) ** -0.5
    BLOCKS = (B * N - E) // P + E
    ROW = 2 * D + 4
    C_PROB, C_TOKEN, C_EXPERT = 2 * D, 2 * D + 1, 2 * D + 2
    NO_TOKEN = 1 << 20
    RING = 8
    BLOCKS_PEELED = 2 * RING - 1
    assert (BLOCKS - BLOCKS_PEELED) % RING == 0
    assert D == P and PER_BATCH == 2 and KC == 2 * T

    x_rows = x.rearrange("b n d -> (b n) d")
    x_tiles = x_rows.rearrange("(t p) d -> p t d", p=P)
    out_rows = out.rearrange("b n d -> (b n) d")
    table = nc.dram_tensor("expert_rows", (BLOCKS * P, ROW), F32, kind="Internal").ap()
    table_blocks = table.rearrange("(n p) c -> n p c", p=P)

    with ExitStack() as ctx:
        def sb(name, shape, dt=F32):
            return ctx.enter_context(nc.sbuf_tensor(name, shape, dt))

        def sem(name):
            return ctx.enter_context(nc.semaphore(name))

        x_all = sb("x_all", [P, GROUPS * T, D])
        keysT = sb("keysT", [P, 2, B * N], F32R)
        values = sb("values", [P, KC, D])
        probs = sb("probs", [P, 2 * T * N])
        qT = sb("qT", [P, 2, 2, G], F32R)
        probsT = sb("probsT", [P, 2, G])
        xn = sb("xn", [P, 2, T, D])
        mixedT = sb("mixedT", [P, 2, G])
        pay = sb("pay", [P, 2, T, ROW])
        pay_i = pay[:, :, :, :].bitcast(I32)
        xn2T = sb("xn2T", [P, G])
        w1_sb = sb("w1_sb", [P, E, H])
        w2_sb = sb("w2_sb", [P, E, HC, D])
        b1_rep = sb("b1_rep", [P, E, H])
        b2_rep = sb("b2_rep", [P, E, D])
        wq_sb = sb("wq_sb", [P, D])
        wk_sb = sb("wk_sb", [P, D])
        wv_sb = sb("wv_sb", [P, D])
        wvT = sb("wvT", [P, D])
        m_hl = sb("m_hl", [P, 2, D], F32R)
        wr_sb = sb("wr_sb", [P, E])
        br_rep = sb("br_rep", [P, E])
        ident = sb("ident", [P, P])
        before_f = sb("before_f", [P, P])
        before = sb("before", [P, P], BF16)
        ones = sb("ones", [P, P], BF16)
        descend = sb("descend", [P, E])
        steps128 = sb("steps128", [P, T, E])
        tokens = sb("tokens", [P, GROUPS * T], I32)
        experts_of = sb("experts_of", [1, BLOCKS], I32)
        pad_rows = sb("pad_rows", [P, ROW])
        row_sum = sb("row_sum", [P, 2, T])
        weight = sb("weight", [P, 2, T])
        neg_max = sb("neg_max", [P, 2, T])
        stats1 = sb("stats1", [P, T, 6])
        mv1 = sb("mv1", [P, T, 2])
        rstd1 = sb("rstd1", [P, T])
        shift1 = sb("shift1", [P, T])
        stats2 = sb("stats2", [P, T, 6])
        mv2 = sb("mv2", [P, T, 2])
        newton = sb("newton", [P, 3, T])
        minus_half = sb("minus_half", [P, T])
        rstd2 = sb("rstd2", [P, T])
        shift2 = sb("shift2", [P, T])
        logit = sb("logit", [P, T, E])
        logit_max = sb("logit_max", [P, T])
        below = sb("below", [P, T, E])
        rank_key = sb("rank_key", [P, T, E])
        best_key = sb("best_key", [P, T])
        exps = sb("exps", [P, T, E])
        exp_sum = sb("exp_sum", [P, T])
        chosen = sb("chosen", [P, 2, T, E])
        chosen_b = sb("chosen_b", [P, T, E], BF16)
        counts = sb("counts", [P, T + 1, E])
        cap = sb("cap", [P, E])
        nxt = sb("nxt", [P, E])
        need = sb("need", [P, E])
        over = sb("over", [P, T, E])
        over2 = sb("over2", [P, 2, E])
        scan = sb("scan", [P, 4, 2 * E])
        fresh = sb("fresh", [P, E])
        delta = sb("delta", [P, E])
        moved = sb("moved", [P, E])
        room = sb("room", [P, E])
        place = sb("place", [P, T, E])
        place4 = sb("place4", [P, T, 4])
        place2 = sb("place2", [P, T, 2])
        place1 = sb("place1", [P, T])
        position = sb("position", [P, 2, T], I32)

        def probs_tile(parity, j):
            at = (parity * T + j) * N
            return probs[:, at:at + N]

        at = [0]

        def carve(n):
            at[0] += n
            return probs[:, at[0] - n:at[0]]

        block_in = [carve(ROW) for _ in range(RING)]
        block_T = [carve(P) for _ in range(2)]
        block_token = [carve(1).bitcast(I32) for _ in range(RING)]
        hidden = [carve(H) for _ in range(2)]
        hiddenT = [carve(H) for _ in range(2)]
        block_y = [carve(D) for _ in range(2)]
        block_out = [carve(D) for _ in range(RING)]

        ps_s = [ctx.enter_context(nc.psum_tensor(f"ps_s{n}", [P, N], F32)) for n in range(2)]
        ps_t = [ctx.enter_context(nc.psum_tensor(f"ps_t{n}", [P, G], F32)) for n in range(2)]
        ps_u = ctx.enter_context(nc.psum_tensor("ps_u", [P, G], F32))
        ps_m = ctx.enter_context(nc.psum_tensor("ps_m", [P, G], F32))

        x_in = [sem(f"x_in{n}") for n in range(3)]
        qk_in = sem("qk_in")
        v_in = sem("v_in")
        router_in = sem("router_in")
        experts_in = sem("experts_in")
        consts = sem("consts")
        half_ready = sem("half_ready")
        passed = sem("passed")
        pads_ready = sem("pads_ready")
        ident_ready = sem("ident_ready")
        m_psum = sem("m_psum")
        m_hi = sem("m_hi")
        m_lo = sem("m_lo")
        wvT_psum = sem("wvT_psum")
        wvT_ready = sem("wvT_ready")
        ln1 = sem("ln1")
        scale1 = sem("scale1")
        xn_ready = sem("xn_ready")
        xT_psum = sem("xT_psum")
        xT_hi = sem("xT_hi")
        xT_lo = sem("xT_lo")
        q_psum = sem("q_psum")
        q_hi = sem("q_hi")
        q_lo = sem("q_lo")
        values_in = [sem(f"values_in{n}") for n in range(2)]
        s_psum = sem("s_psum")
        max_ready = sem("max_ready")
        exp_ready = sem("exp_ready")
        weight_ready = sem("weight_ready")
        pT_psum = sem("pT_psum")
        pT_copied = [sem(f"pT_copied{n}") for n in range(2)]
        mixed = sem("mixed")
        mixedT_ready = sem("mixedT_ready")
        att_psum = sem("att_psum")
        x1_ready = sem("x1_ready")
        ln2 = sem("ln2")
        xn2_ready = sem("xn2_ready")
        xn2T_psum = sem("xn2T_psum")
        xn2T_ready = sem("xn2T_ready")
        logit_psum = sem("logit_psum")
        pick = sem("pick")
        exps_ready = sem("exps_ready")
        prob_ready = sem("prob_ready")
        chosen_ready = sem("chosen_ready")
        counts_psum = sem("counts_psum")
        counts_ready = sem("counts_ready")
        numbered = sem("numbered")
        route = sem("route")
        rows_out = [sem(f"rows_out{n}") for n in range(2)]
        experts_known = sem("experts_known")
        b_in = [sem(f"b_in{n}") for n in range(RING)]
        b_x_psum = sem("b_x_psum")
        b_xT = sem("b_xT")
        b_token = sem("b_token")
        b_up = sem("b_up")
        b_hidden = sem("b_hidden")
        b_t_psum = sem("b_t_psum")
        b_relu = sem("b_relu")
        b_down = sem("b_down")
        b_biased = sem("b_biased")
        b_done = sem("b_done")
        b_out = [sem(f"b_out{n}") for n in range(RING)]

        def wait(eng, s, value):
            if not isinstance(value, int) or value > 0:
                eng.wait_ge(s, value)

        def apart(eng):
            eng.sem_inc(passed, 1)

        def parts(s, b):
            found = [2 * b + s + d for d in (0, -1, -2, 2, 1)]
            found = [v if not isinstance(v, int) or 0 <= v < GROUPS else None for v in found]
            return found

        def ps_att(r):
            return ps_s[0] if is_last(r) else ps_m

        def is_first(g):
            return isinstance(g, int) and g == 0

        def is_last(r):
            return isinstance(r, int) and r == GROUPS - 1

        LAST = GROUPS + 2
        LOOP_FROM, LOOP_TO = 1, (GROUPS - 2) // 2

        def pipeline(eng, step):
            for i in range(2 * LOOP_FROM):
                step(i % 2, i // 2)
            with eng.Fori(LOOP_FROM, LOOP_TO) as b:
                for s in range(2):
                    step(s, b)
            for i in range(2 * LOOP_TO, LAST):
                step(i % 2, i // 2)

        LN1_STEPS = 2 * T
        LN2_STEPS = 2 * T + 13
        PICK_STEPS = 6
        CONSTS = 4 + E + T + 1 + 3 + 1

        ps_in = lambda a: (ps_u, ps_m)[a % 2][:, 0:P]
        ps_up = lambda a: ps_s[a % 2][:, 0:H]
        ps_hidden = lambda a: ps_s[a % 2][:, G:G + H]
        ps_down = lambda a: ps_t[a % 2][:, 0:D]

        def number(a, n):
            return a + RING * n

        def uses(a, n):
            return a // RING + n

        def experts_from(engine, at, count):
            cells = experts_of[0:1, bass.ds(at, count)]
            return nc.values_load_multi_w_load_instructions(
                cells, engines=[engine], min_val=0, max_val=E - 1,
                skip_runtime_bounds_check_because="each is an index among E experts, or a padding row's 0")[1]

        def blocks(eng, step, engine=None):
            def rounds(first, last, n):
                at = max(first - 3, 0)
                known = engine and experts_from(engine, number(at, n), last - at)
                for a in range(first, last):
                    step(a, n, known and [known[max(a - d, 0) - at] for d in (3, 2, 1, 0)])

            rounds(0, RING, 0)
            rounds(RING, BLOCKS_PEELED, 0)
            with eng.Fori(0, (BLOCKS - BLOCKS_PEELED) // RING) as n:
                rounds(BLOCKS_PEELED, BLOCKS_PEELED + RING, n)

        block = ctx.enter_context(nc.Block())

        @block.sync
        def _(sp):
            sp.dma_start(x_all[:, 0:T, :], x_tiles[:, 0:T, :]).then_inc(x_in[0], 16)
            sp.dma_start(wq_sb[:, :], Wq).then_inc(qk_in, 16)
            sp.dma_start(wk_sb[:, :], Wk).then_inc(qk_in, 16)
            sp.dma_start(x_all[:, T:2 * T, :], x_tiles[:, T:2 * T, :]).then_inc(x_in[1], 16)
            sp.dma_start(wv_sb[:, :], Wv).then_inc(v_in, 16)
            sp.dma_start(wr_sb[:, :], w_router).then_inc(router_in, 16)
            sp.dma_start(br_rep[:, :], b_router.partition_broadcast(P)).then_inc(router_in, 16)
            sp.dma_start(x_all[:, 2 * T:, :], x_tiles[:, 2 * T:, :]).then_inc(x_in[2], 16)

            def load_values(b):
                for h in range(2):
                    sp.wait_ge(xn_ready, T * (2 * b + h + 1))
                    apart(sp)
                    wait(sp, mixed, KC * (2 * b - 1) + T * h + T)
                    apart(sp)
                    sp.dma_start(values[:, T * h:T * h + T, :], xn[:, h, :, :]).then_inc(values_in[h], 16)

            load_values(0)
            sp.dma_start(w1_sb[:, :, :], w1.rearrange("e d h -> d e h")).then_inc(experts_in, 16)
            for c in range(HC):
                sp.dma_start(w2_sb[:, :, c, :], w2[:, c * P:(c + 1) * P, :].rearrange("e p d -> p e d"))\
                  .then_inc(experts_in, 16)
            sp.dma_start(b1_rep[:, :, :], b1.partition_broadcast(P)).then_inc(experts_in, 16)
            sp.dma_start(b2_rep[:, :, :], b2.partition_broadcast(P)).then_inc(experts_in, 16)
            with sp.Fori(1, B) as b:
                load_values(b)

            for n in range(2):
                sp.wait_ge(rows_out[n], 16 + 16 * T * GROUPS // 2)
            sp.wait_ge(pT_psum, KC * GROUPS)

            first_rows = table_blocks[:, 0, C_EXPERT:C_EXPERT + 1].rearrange("n c -> c n")
            sp.dma_start(experts_of[0:1, :], first_rows.bitcast(I32),
                         allow_slow_non_contiguous=True).then_inc(experts_known, 16)

            def load_block(a, n, _):
                free = number(a, n) + 1 - RING
                wait(sp, b_done, free)
                apart(sp)
                wait(sp, b_token, free)
                apart(sp)
                rows = table_blocks[bass.ds(number(a, n), 1), :, :].rearrange("n p c -> p (n c)")
                sp.dma_start(block_in[a % RING], rows).then_inc(b_in[a % RING], 16)

            blocks(sp, load_block)
            for n in range(RING):
                sp.wait_ge(b_out[n], 16 * len(range(n, BLOCKS, RING)))

        @block.gpsimd
        def _(pool):
            pool.memset(ident[:, :], 0.0).then_inc(ident_ready, 1)
            pool.wait_ge(ident_ready, 1)
            pool.affine_select(out=ident[:, :], in_=ident[:, :], compare_op=ALU.not_equal, fill=1.0,
                               base=0, pattern=[[-1, P]], channel_multiplier=1).then_inc(ident_ready, 1)
            pool.memset(minus_half[:, :], -0.5).then_inc(half_ready, 1)
            pool.wait_ge(half_ready, 1)

            def scale_rows(k):
                pool.wait_ge(ln1, LN1_STEPS * k + LN1_STEPS)
                wait(pool, xn_ready, T * k)
                apart(pool)
                pool.tensor_scalar(rstd1[:, :], mv1[:, :, 1], EPS, None, ALU.add).then_inc(scale1, 1)
                pool.wait_ge(scale1, 4 * k + 1)
                pool.tensor_tensor(rstd1[:, :], rstd1[:, :], minus_half[:, :], ALU.pow).then_inc(scale1, 1)
                pool.wait_ge(scale1, 4 * k + 2)
                pool.tensor_tensor(shift1[:, :], mv1[:, :, 0], rstd1[:, :], ALU.mult).then_inc(scale1, 1)
                pool.wait_ge(scale1, 4 * k + 3)
                apart(pool)
                pool.tensor_scalar(shift1[:, :], shift1[:, :], -1.0, None, ALU.mult).then_inc(scale1, 1)

            for k in range(2):
                scale_rows(k)
            pool.memset(pad_rows[:, :], 0.0).then_inc(pads_ready, 1)
            pool.wait_ge(pads_ready, 1)
            pool.memset(pad_rows[:, C_TOKEN:C_TOKEN + 1].bitcast(I32), NO_TOKEN).then_inc(pads_ready, 1)
            pool.wait_ge(pads_ready, 2)
            table_columns = table.rearrange("(n p) c -> p n c", p=P)
            for n, (lo, hi) in enumerate(((0, BLOCKS // 2), (BLOCKS // 2, BLOCKS))):
                pool.dma_start(table_columns[:, lo:hi, :],
                             pad_rows[:, :].unsqueeze(1).to_broadcast([P, hi - lo, ROW])).then_inc(rows_out[n], 16)
            pool.memset(before_f[:, :], 1.0).then_inc(consts, 1)
            pool.wait_ge(consts, 1)
            pool.affine_select(out=before_f[:, :], in_=before_f[:, :], compare_op=ALU.is_gt, fill=0.0,
                               base=0, pattern=[[1, P]], channel_multiplier=-1).then_inc(consts, 1)
            pool.wait_ge(consts, 2)
            pool.tensor_copy(before[:, :], before_f[:, :]).then_inc(consts, 1)
            pool.memset(ones[:, :], 1.0).then_inc(consts, 1)
            for e in range(E):
                pool.memset(descend[:, e:e + 1], float(E - e)).then_inc(consts, 1)
            for j in range(T):
                pool.memset(steps128[:, j, :], float(P * j)).then_inc(consts, 1)
            pool.iota(tokens[:, :], pattern=[[P, GROUPS * T]], base=0, channel_multiplier=1).then_inc(consts, 1)
            for state in (cap, nxt, scan):
                pool.memset(state[:], 0.0).then_inc(consts, 1)
            pool.memset(pay[:, :, :, ROW - 1:ROW], 0.0).then_inc(consts, 1)
            pool.wait_ge(consts, CONSTS)

            def number_rows(r, s, b):
                wait(pool, rows_out[s], 16 + (b - 1) * 16 * T)
                apart(pool)
                pool.tensor_copy(pay_i[:, s, :, C_TOKEN], tokens[:, bass.ds(r * T, T)]).then_inc(numbered, 1)
                pool.wait_ge(pick, PICK_STEPS * r + 5)
                apart(pool)
                pool.tensor_scalar(pay_i[:, s, :, C_EXPERT], best_key[:, :], -1.0, float(E),
                                   ALU.mult, ALU.add).then_inc(numbered, 1)

            def place_rows(r, s):
                done = [0]

                def then(ins, alone=False):
                    done[0] += 1
                    ins.then_inc(route, 1)
                    pool.wait_ge(route, r * ROUTE_STEPS + done[0])
                    if alone:
                        apart(pool)

                over_tiles = lambda v: v.unsqueeze(1).to_broadcast([P, T, E])
                tt = pool.tensor_tensor
                total = counts[:, T, :]
                ranks = counts[:, 0:T, :]
                pool.wait_ge(counts_ready, r + 1)
                pool.wait_ge(pick, PICK_STEPS * r + 6)
                then(tt(need[:, :], total, cap[:, :], ALU.subtract))
                then(tt(over[:, :, :], over_tiles(need[:, :]), steps128[:, :, :], ALU.subtract), alone=True)
                then(pool.tensor_scalar(over[:, :, :], over[:, :, :], 0.0, None, ALU.is_gt))
                then(tt(over2[:, :, :], over[:, 0:2, :], over[:, 2:4, :], ALU.add))
                then(tt(scan[:, 0, E:2 * E], over2[:, 0, :], over2[:, 1, :], ALU.add))
                for n in range(3):
                    then(tt(scan[:, n + 1, E - 1:2 * E], scan[:, n, E - 1:2 * E],
                            scan[:, n, E - 1 - (1 << n):2 * E - (1 << n)], ALU.add), alone=True)
                then(pool.tensor_scalar(fresh[:, :], scan[:, 3, E - 1:2 * E - 1], float(P), None, ALU.mult))
                then(tt(fresh[:, :], fresh[:, :], cap[:, :], ALU.subtract))
                then(tt(delta[:, :], fresh[:, :], nxt[:, :], ALU.subtract))
                then(tt(place[:, :, :], ranks, over_tiles(cap[:, :]), ALU.subtract), alone=True)
                then(pool.tensor_scalar(place[:, :, :], place[:, :, :], 0.0, None, ALU.is_ge))
                then(tt(place[:, :, :], place[:, :, :], over_tiles(delta[:, :]), ALU.mult))
                then(tt(place[:, :, :], place[:, :, :], ranks, ALU.add))
                then(tt(place[:, :, :], place[:, :, :], over_tiles(nxt[:, :]), ALU.add))
                then(tt(place[:, :, :], place[:, :, :], chosen[:, s, :, :], ALU.mult))
                then(tt(place4[:, :, :], place[:, :, 0:4], place[:, :, 4:8], ALU.add))
                then(tt(place2[:, :, :], place4[:, :, 0:2], place4[:, :, 2:4], ALU.add))
                then(tt(place1[:, :], place2[:, :, 0], place2[:, :, 1], ALU.add), alone=True)
                then(pool.tensor_copy(position[:, s, :], place1[:, :]))
                apart(pool)
                pool.wait_ge(numbered, 2 * r + 2)
                pool.wait_ge(xn2_ready, T * r + T)
                pool.wait_ge(x1_ready, T * r + T)
                pool.wait_ge(prob_ready, 2 * r + 2)
                apart(pool)
                for j in range(T):
                    pool.indirect_dma_start(
                        out=table[:, :], out_offset=bass.IndirectOffsetOnAxis(ap=position[:, s, j:j + 1], axis=0),
                        in_=pay[:, s, j, :], in_offset=None,
                        bounds_check=BLOCKS * P - 1, oob_is_err=False).then_inc(rows_out[s], 16)
                then(tt(moved[:, :], over[:, 0, :], delta[:, :], ALU.mult))
                then(tt(nxt[:, :], nxt[:, :], moved[:, :], ALU.add))
                then(tt(nxt[:, :], nxt[:, :], total, ALU.add), alone=True)
                then(pool.tensor_scalar(room[:, :], scan[:, 0, E:2 * E], float(P), None, ALU.mult))
                then(tt(cap[:, :], room[:, :], need[:, :], ALU.subtract))
                then(tt(scan[:, 0, E - 1:E], scan[:, 0, E - 1:E], scan[:, 3, 2 * E - 1:2 * E], ALU.add))
                assert done[0] == ROUTE_STEPS

            def step(s, b):
                g, p, r, k, u = parts(s, b)
                if k is not None:
                    scale_rows(k)
                if r is not None:
                    number_rows(r, s, b)
                if r is not None:
                    place_rows(r, s)
                elif s == 1:
                    for n in range(2):
                        pool.wait_ge(rows_out[n], 16)

            pipeline(pool, step)

            def scatter_block(a, n, _):
                pool.wait_ge(b_done, number(a, n) + 1)
                apart(pool)
                pool.wait_ge(b_token, number(a, n) + 1)
                apart(pool)
                pool.indirect_dma_start(
                    out=out_rows, in_=block_out[a % RING], in_offset=None,
                    out_offset=bass.IndirectOffsetOnAxis(
                        ap=block_token[a % RING], axis=0),
                    bounds_check=B * N - 1, oob_is_err=False).then_inc(b_out[a % RING], 16)

            blocks(pool, scatter_block)

        @block.vector
        def _(dve):
            tt = dve.tensor_tensor

            def stats(src, bn, mv, count, base, part):
                if part in (0, None):
                    for j in range(T):
                        dve.bn_stats(out=bn[:, j, :], in_=src(j)).then_inc(count, 1)
                if part in (1, None):
                    for j in range(T):
                        dve.wait_ge(count, base + j + 1)
                        apart(dve)
                        dve.bn_aggr(out=mv[:, j, :], in_=bn[:, j, :]).then_inc(count, 1)

            def stats1_of(k, s, part=None):
                if part in (0, None):
                    if isinstance(k, int) and k < 2:
                        dve.wait_ge(x_in[k], 16)
                    else:
                        dve.wait_ge(x_in[2], 16)
                    wait(dve, scale1, 4 * k)
                stats(lambda j: x_all[:, bass.ds(k * T + j, 1), :].rearrange("p a d -> p (a d)"),
                      stats1, mv1, ln1, LN1_STEPS * k, part)

            def xT_lo_of(k, ps=ps_m):
                dve.wait_ge(xT_hi, k + 1)
                cols = bass.ds(k * G, G)
                tt(keysT[:, 1, cols], ps[:, :], keysT[:, 0, cols].bitcast(F32), ALU.subtract).then_inc(xT_lo, 1)

            def q_lo_of(k, s):
                dve.wait_ge(q_hi, k + 1)
                tt(qT[:, s, 1, :], ps_m[:, :], qT[:, s, 0, :].bitcast(F32), ALU.subtract).then_inc(q_lo, 1)

            stats1_of(0, 0)
            dve.wait_ge(m_hi, 1)
            tt(m_hl[:, 1, :], ps_t[0][:, 0:D], m_hl[:, 0, :].bitcast(F32), ALU.subtract).then_inc(m_lo, 1)
            stats1_of(1, 1)
            xT_lo_of(0)
            q_lo_of(0, 0)
            xT_lo_of(1, ps_u)

            def step(s, b):
                g, p, r, k, u = parts(s, b)
                q = 1 - s

                def row_max(j):
                    if g is None:
                        return
                    dve.wait_ge(s_psum, T * g + j + 1)
                    wait(dve, exp_ready, T * (g - 2) + j + 1)
                    dve.tensor_reduce(out=neg_max[:, s, j:j + 1], in_=ps_s[j % 2][:, :], axis=AX.X,
                                      op=ALU.max, negate=True).then_inc(max_ready, 1)

                def evacuate(c):
                    if p is None:
                        return
                    dve.wait_ge(pT_psum, KC * p + c + 1)
                    wait(dve, mixed, KC * p + c - 1)
                    dve.tensor_copy(probsT[:, c % 2, :], ps_t[c % 2][:, :]).then_inc(pT_copied[c % 2], 1)

                def weights():
                    dve.wait_ge(exp_ready, T * p + T)
                    dve.reciprocal(weight[:, q, :], row_sum[:, q, :]).then_inc(weight_ready, 1)
                    dve.wait_ge(weight_ready, 2 * p + 1)
                    dve.tensor_scalar(weight[:, q, :], weight[:, q, :], NORM, None, ALU.mult)\
                       .then_inc(weight_ready, 1)

                def residual(j):
                    if j == 0:
                        dve.wait_ge(att_psum, r + 1)
                        dve.wait_ge(weight_ready, 2 * r + 2)
                        wait(dve, rows_out[s], 16 + (b - 1) * 16 * T)
                    dve.scalar_tensor_tensor(
                        pay[:, s, j, D:2 * D], ps_att(r)[:, j * D:(j + 1) * D], weight[:, s, j:j + 1],
                        x_all[:, bass.ds(r * T + j, 1), :].rearrange("p a d -> p (a d)"),
                        ALU.mult, ALU.add).then_inc(x1_ready, 1)

                def stats2_of(part):
                    if part == 0:
                        dve.wait_ge(x1_ready, T * r + T)
                        wait(dve, xn2_ready, T * r)
                    stats(lambda j: pay[:, s, j, D:2 * D], stats2, mv2, ln2, LN2_STEPS * r, part)

                def scale2():
                    done = [2 * T]

                    def then(ins):
                        done[0] += 1
                        ins.then_inc(ln2, 1)
                        if done[0] < LN2_STEPS:
                            dve.wait_ge(ln2, LN2_STEPS * r + done[0])

                    bits = newton[:, 1, :].bitcast(I32)
                    dve.wait_ge(ln2, LN2_STEPS * r + 2 * T)
                    then(dve.tensor_scalar(newton[:, 0, :], mv2[:, :, 1], EPS, None, ALU.add))
                    then(dve.tensor_scalar(bits, newton[:, 0, :].bitcast(I32), 1, None, ALU.logical_shift_right))
                    then(dve.tensor_scalar(rstd2[:, :].bitcast(I32), bits, -1.0, float(0x5f3759df),
                                           ALU.mult, ALU.add))
                    for n in range(3):
                        then(tt(newton[:, 1, :], rstd2[:, :], rstd2[:, :], ALU.mult))
                        then(dve.scalar_tensor_tensor(newton[:, 2, :], newton[:, 1, :], -0.5, newton[:, 0, :],
                                                      ALU.mult, ALU.mult))
                        then(dve.scalar_tensor_tensor(rstd2[:, :], newton[:, 2, :], 1.5, rstd2[:, :],
                                                      ALU.add, ALU.mult))
                    then(dve.scalar_tensor_tensor(shift2[:, :], mv2[:, :, 0], -1.0, rstd2[:, :],
                                                  ALU.mult, ALU.mult))
                    assert done[0] == LN2_STEPS

                def choose():
                    per_expert = lambda v: v.unsqueeze(2).to_broadcast([P, T, E])
                    over_tiles = lambda v: v.unsqueeze(1).to_broadcast([P, T, E])
                    dve.wait_ge(logit_psum, r + 1)
                    tt(logit[:, :, :], ps_m[:, 0:T * E].rearrange("p (t e) -> p t e", e=E),
                       over_tiles(br_rep[:, :]), ALU.add).then_inc(pick, 1)
                    dve.wait_ge(pick, PICK_STEPS * r + 1)
                    dve.tensor_reduce(out=logit_max[:, :], in_=logit[:, :, :], axis=AX.X,
                                      op=ALU.max).then_inc(pick, 1)
                    dve.wait_ge(pick, PICK_STEPS * r + 2)
                    wait(dve, exps_ready, r)
                    tt(below[:, :, :], logit[:, :, :], per_expert(logit_max[:, :]), ALU.subtract)\
                        .then_inc(pick, 1)
                    dve.wait_ge(pick, PICK_STEPS * r + 3)
                    wait(dve, numbered, 2 * r)
                    dve.scalar_tensor_tensor(rank_key[:, :, :], below[:, :, :], 0.0, over_tiles(descend[:, :]),
                                             ALU.is_ge, ALU.mult).then_inc(pick, 1)
                    dve.wait_ge(pick, PICK_STEPS * r + 4)
                    dve.tensor_reduce(out=best_key[:, :], in_=rank_key[:, :, :], axis=AX.X,
                                      op=ALU.max).then_inc(pick, 1)
                    dve.wait_ge(pick, PICK_STEPS * r + 5)
                    wait(dve, counts_psum, r)
                    tt(chosen_b[:, :, :], rank_key[:, :, :], per_expert(best_key[:, :]), ALU.is_equal)\
                        .then_inc(chosen_ready, 1)
                    tt(chosen[:, s, :, :], rank_key[:, :, :], per_expert(best_key[:, :]), ALU.is_equal)\
                        .then_inc(pick, 1)

                def probability():
                    dve.wait_ge(exps_ready, r + 1)
                    dve.reduce_sum(exp_sum[:, :], exps[:, :, :], axis=AX.X).then_inc(prob_ready, 1)
                    dve.wait_ge(prob_ready, 2 * r + 1)
                    dve.reciprocal(pay[:, s, :, C_PROB], exp_sum[:, :]).then_inc(prob_ready, 1)

                if is_first(g):
                    stats1_of(k, s)
                    row_max(0)
                    row_max(1)
                    q_lo_of(u, q)
                    xT_lo_of(k)
                    row_max(2)
                    row_max(3)
                    dve.wait_ge(router_in, 32)
                    dve.wait_ge(consts, CONSTS)
                    return
                evacuate(0)
                if k is not None:
                    stats1_of(k, s)
                row_max(0)
                if p is not None:
                    weights()
                if r is not None:
                    for j in range(T):
                        residual(j)
                evacuate(2)
                if r is not None:
                    stats2_of(0)
                    stats2_of(1)
                row_max(1)
                if r is not None:
                    scale2()
                if u is not None:
                    q_lo_of(u, q)
                row_max(2)
                evacuate(6)
                if r is not None:
                    choose()
                row_max(3)
                if r is not None:
                    probability()
                if k is not None:
                    xT_lo_of(k)

            pipeline(dve, step)

            dve.wait_ge(experts_in, 16 * (3 + HC))

            def hidden_of(a, n, expert):
                t = number(a, n)
                dve.wait_ge(b_up, t + 1)
                wait(dve, b_t_psum, t - 1)
                tt(hidden[a % 2], ps_up(a), b1_rep[:, bass.ds(expert, 1), :].rearrange("p a h -> p (a h)"),
                   ALU.add).then_inc(b_hidden, 1)

            def output_of(a, n, expert):
                t = number(a, n)
                rows = block_in[a % RING]
                dve.wait_ge(b_down, t + 1)
                dve.wait_ge(b_in[a % RING], 16 * (uses(a, n) + 1))
                tt(block_y[a % 2], ps_down(a), b2_rep[:, bass.ds(expert, 1), :].rearrange("p a d -> p (a d)"),
                   ALU.add).then_inc(b_biased, 1)
                dve.wait_ge(b_biased, t + 1)
                wait(dve, b_out[a % RING], 16 * uses(a, n))
                dve.scalar_tensor_tensor(block_out[a % RING], block_y[a % 2], rows[:, C_PROB:C_PROB + 1],
                                         rows[:, D:2 * D], ALU.mult, ALU.add).then_inc(b_done, 1)

            dve.wait_ge(experts_known, 16)

            def block_step(a, n, experts):
                hidden_of(a, n, experts[3])
                if a > 2:
                    output_of(a - 3, n, experts[0])

            blocks(dve, block_step, mybir.EngineType.DVE)
            experts = experts_from(mybir.EngineType.DVE, BLOCKS - 3, 3)
            for d in range(3):
                output_of(BLOCKS - 3 + d, 0, experts[d])

        @block.scalar
        def _(act):
            ln_apply = lambda dst, src, rstd, shift: act.activation(dst, src, ACT.Identity, bias=shift, scale=rstd)

            def norm1(k, s, batch):
                act.wait_ge(scale1, 4 * k + 4)
                wait(act, xT_psum, k - 1)
                wait(act, values_in[s], 16 * batch)
                for j in range(T):
                    ln_apply(xn[:, s, j, :], x_all[:, bass.ds(k * T + j, 1), :].rearrange("p a d -> p (a d)"),
                             rstd1[:, j:j + 1], shift1[:, j:j + 1]).then_inc(xn_ready, 1)

            def xT_hi_of(k, ps=ps_m):
                act.wait_ge(xT_psum, k + 1)
                act.copy(keysT[:, 0, bass.ds(k * G, G)], ps[:, :]).then_inc(xT_hi, 1)

            def q_hi_of(k, s):
                act.wait_ge(q_psum, k + 1)
                wait(act, s_psum, T * (k - 2) + T)
                act.copy(qT[:, s, 0, :], ps_m[:, :]).then_inc(q_hi, 1)

            act.wait_ge(m_psum, 1)
            act.copy(m_hl[:, 0, :], ps_t[0][:, 0:D]).then_inc(m_hi, 1)
            norm1(0, 0, 0)
            xT_hi_of(0)
            norm1(1, 1, 0)
            q_hi_of(0, 0)
            xT_hi_of(1, ps_u)

            def step(s, b):
                g, p, r, k, u = parts(s, b)
                q = 1 - s

                def exponentials(j):
                    if g is None:
                        return
                    act.wait_ge(max_ready, T * g + j + 1)
                    if j == 0:
                        wait(act, pT_psum, KC * (g - 2) + KC)
                        wait(act, weight_ready, 2 * (g - 2) + 2)
                    act.activation(probs_tile(s, j), ps_s[j % 2][:, :], ACT.Exp, bias=neg_max[:, s, j:j + 1],
                                   accum_out=row_sum[:, s, j:j + 1]).then_inc(exp_ready, 1)

                def evacuate(c):
                    if p is None:
                        return
                    act.wait_ge(pT_psum, KC * p + c + 1)
                    wait(act, mixed, KC * p + c - 1)
                    act.copy(probsT[:, c % 2, :], ps_t[c % 2][:, :]).then_inc(pT_copied[c % 2], 1)

                def norm2():
                    act.wait_ge(ln2, LN2_STEPS * r + LN2_STEPS)
                    wait(act, rows_out[s], 16 + (b - 1) * 16 * T)
                    for j in range(T):
                        ln_apply(pay[:, s, j, 0:D], pay[:, s, j, D:2 * D], rstd2[:, j:j + 1],
                                 shift2[:, j:j + 1]).then_inc(xn2_ready, 1)

                def mixed_out(v, parity):
                    act.wait_ge(mixed, KC * v + KC)
                    wait(act, att_psum, v)
                    act.copy(mixedT[:, parity, :], ps_u[:, :]).then_inc(mixedT_ready, 1)

                if r is not None and not is_last(r):
                    mixed_out(r, s)
                if is_first(g):
                    norm1(k, s, b + 1)
                    exponentials(0)
                    q_hi_of(u, q)
                    exponentials(1)
                    xT_hi_of(k)
                    exponentials(2)
                    exponentials(3)
                    act.wait_ge(wvT_psum, 1)
                    act.copy(wvT[:, :], ps_t[1][:, 0:D]).then_inc(wvT_ready, 1)
                    return
                evacuate(1)
                exponentials(0)
                evacuate(3)
                exponentials(1)
                evacuate(4)
                if u is not None:
                    q_hi_of(u, q)
                if g is None:
                    evacuate(5)
                    evacuate(7)
                if r is not None:
                    norm2()
                if g is not None:
                    evacuate(5)
                elif p is not None:
                    mixed_out(p, q)
                if r is not None:
                    act.wait_ge(xn2T_psum, r + 1)
                    wait(act, logit_psum, r)
                    act.copy(xn2T[:, :], ps_m[:, :]).then_inc(xn2T_ready, 1)
                exponentials(2)
                if k is not None:
                    norm1(k, s, b + 1)
                if g is not None:
                    evacuate(7)
                if r is not None:
                    act.wait_ge(pick, PICK_STEPS * r + 3)
                    wait(act, prob_ready, 2 * r)
                    act.activation(exps[:, :, :], below[:, :, :], ACT.Exp).then_inc(exps_ready, 1)
                    act.wait_ge(counts_psum, r + 1)
                    wait(act, route, ROUTE_STEPS * r)
                    act.copy(counts[:, :, :], ps_m[:, 0:(T + 1) * E].rearrange("p (t e) -> p t e", e=E))\
                       .then_inc(counts_ready, 1)
                exponentials(3)
                if k is not None:
                    xT_hi_of(k)

            pipeline(act, step)

            def transposed(a, n):
                t = number(a, n)
                act.wait_ge(b_x_psum, t + 1)
                wait(act, b_up, t - 1)
                act.copy(block_T[a % 2], ps_in(a)).then_inc(b_xT, 1)

            def tokens_of(a, n):
                act.wait_ge(b_in[a % RING], 16 * (uses(a, n) + 1))
                wait(act, b_out[a % RING], 16 * uses(a, n))
                apart(act)
                act.copy(block_token[a % RING], block_in[a % RING][:, C_TOKEN:C_TOKEN + 1].bitcast(I32))\
                   .then_inc(b_token, 1)

            def relu(a, n):
                t = number(a, n)
                act.wait_ge(b_t_psum, t + 1)
                wait(act, b_down, t - 1)
                act.activation(hiddenT[a % 2], ps_hidden(a), ACT.Relu).then_inc(b_relu, 1)

            def block_step(a, n, _):
                transposed(a, n)
                if a > 1:
                    relu(a - 2, n)
                tokens_of(a, n)

            blocks(act, block_step)
            for a in (BLOCKS - 2, BLOCKS - 1):
                relu(a, 0)

        @block.tensor
        def _(pe):
            HI_LO = ((0, 0), (0, 1), (1, 0))

            def transpose_rows(k, s, ps=ps_m):
                pe.wait_ge(xn_ready, T * k + T)
                for j in range(T):
                    last = pe.transpose(ps[:, j * P:(j + 1) * P], xn[:, s, j, :], ident[:, :])
                last.then_inc(xT_psum, 1)

            def queries(k):
                pe.wait_ge(xT_lo, k + 1)
                for n, (wh, xh) in enumerate(HI_LO):
                    last = pe.matmul(ps_m[:, :], m_hl[:, wh, :], keysT[:, xh, bass.ds(k * G, G)],
                                     start=(n == 0), stop=(n == 2))
                last.then_inc(q_psum, 1)

            pe.wait_ge(qk_in, 32)
            pe.matmul(ps_t[0][:, 0:D], wq_sb[:, :], wk_sb[:, :], start=True, stop=True).then_inc(m_psum, 1)
            pe.wait_ge(ident_ready, 2)
            pe.wait_ge(v_in, 16)
            pe.transpose(ps_t[1][:, 0:D], wv_sb[:, :], ident[:, :]).then_inc(wvT_psum, 1)
            transpose_rows(0, 0)
            pe.wait_ge(m_lo, 1)
            queries(0)
            transpose_rows(1, 1, ps_u)

            def step(s, b):
                g, p, r, k, u = parts(s, b)
                q = 1 - s

                def logits(j):
                    if g is None:
                        return
                    if j == 0:
                        pe.wait_ge(q_lo, g + 1)
                        pe.wait_ge(xT_lo, PER_BATCH * (b + 1))
                    wait(pe, exp_ready, T * g + j - 1)
                    for n, (qh, kh) in enumerate(HI_LO):
                        for h in range(N // G):
                            last = pe.matmul(ps_s[j % 2][:, h * G:(h + 1) * G], qT[:, s, qh, j * P:(j + 1) * P],
                                             keysT[:, kh, bass.ds(b * N + h * G, G)],
                                             start=(n == 0), stop=(n == 2))
                    last.then_inc(s_psum, 1)

                def transposes(c):
                    if p is None:
                        return
                    if c == 0:
                        pe.wait_ge(exp_ready, T * p + T)
                    wait(pe, pT_copied[c % 2], T * p + c // 2)
                    for j in range(T):
                        last = pe.transpose(ps_t[c % 2][:, j * P:(j + 1) * P],
                                            probs_tile(q, j)[:, c * P:(c + 1) * P], ident[:, :])
                    last.then_inc(pT_psum, 1)

                def mix(c):
                    if p is None:
                        return
                    if c % T == 0:
                        pe.wait_ge(values_in[c // T], 16 * (b + 1 - q))
                    if c == 0:
                        wait(pe, mixedT_ready, p)
                    pe.wait_ge(pT_copied[c % 2], T * p + c // 2 + 1)
                    pe.matmul(ps_u[:, :], values[:, c, :], probsT[:, c % 2, :],
                              start=(c == 0), stop=(c == KC - 1)).then_inc(mixed, 1)

                def attend(v, parity):
                    pe.wait_ge(mixedT_ready, v + 1)
                    if is_last(v):
                        pe.wait_ge(exp_ready, T * GROUPS)
                    else:
                        wait(pe, counts_ready, v)
                        pe.wait_ge(xT_lo, k if k is not None else GROUPS)
                    for j in range(T):
                        last = pe.matmul(ps_att(v)[:, j * D:(j + 1) * D],
                                         mixedT[:, parity, j * P:(j + 1) * P], wvT[:, :],
                                         start=True, stop=True)
                    last.then_inc(att_psum, 1)

                def transpose_xn2():
                    pe.wait_ge(xn2_ready, T * r + T)
                    pe.wait_ge(x1_ready, T * r + T)
                    if is_last(r):
                        pe.wait_ge(counts_ready, r)
                    pe.wait_ge(q_lo, GROUPS if u is None else u + 1)
                    for j in range(T):
                        last = pe.transpose(ps_m[:, j * P:(j + 1) * P], pay[:, s, j, 0:D], ident[:, :])
                    last.then_inc(xn2T_psum, 1)

                def router():
                    pe.wait_ge(xn2T_ready, r + 1)
                    for j in range(T):
                        last = pe.matmul(ps_m[:, j * E:(j + 1) * E], xn2T[:, j * P:(j + 1) * P], wr_sb[:, :],
                                         start=True, stop=True)
                    last.then_inc(logit_psum, 1)

                def count():
                    pe.wait_ge(pick, PICK_STEPS * r + 1)
                    pe.wait_ge(chosen_ready, r + 1)
                    for j in range(T + 1):
                        out_j = ps_m[:, j * E:(j + 1) * E]
                        for i in range(min(j, T)):
                            last = pe.matmul(out_j, ones[:, :], chosen_b[:, i, :], start=(i == 0),
                                             stop=(j == T and i == T - 1))
                        if j < T:
                            last = pe.matmul(out_j, before[:, :], chosen_b[:, j, :], start=(j == 0), stop=True)
                    last.then_inc(counts_psum, 1)

                if is_first(g):
                    logits(0)
                    logits(1)
                    queries(u)
                    pe.wait_ge(q_lo, u + 1)
                    transpose_rows(k, s)
                    logits(2)
                    logits(3)
                    pe.wait_ge(wvT_ready, 1)
                    pe.wait_ge(router_in, 32)
                    pe.wait_ge(consts, CONSTS)
                    return
                transposes(0)
                logits(0)
                transposes(1)
                mix(0)
                if r is not None and not is_last(r):
                    attend(r, s)
                transposes(2)
                mix(1)
                logits(1)
                transposes(3)
                mix(2)
                transposes(4)
                mix(3)
                if u is not None:
                    if r is not None:
                        pe.wait_ge(x1_ready, T * r + T)
                    queries(u)
                logits(2)
                transposes(5)
                mix(4)
                if g is None and p is not None:
                    transposes(6)
                    mix(5)
                    transposes(7)
                    mix(6)
                    mix(7)
                    transpose_xn2()
                    attend(p, q)
                    router()
                    count()
                    return
                if r is not None:
                    transpose_xn2()
                transposes(6)
                mix(5)
                if r is not None:
                    router()
                logits(3)
                transposes(7)
                if r is not None:
                    count()
                mix(6)
                if k is not None:
                    if r is not None:
                        pe.wait_ge(counts_ready, r + 1)
                    pe.wait_ge(q_lo, u + 1)
                    transpose_rows(k, s)
                mix(7)

            pipeline(pe, step)

            pe.wait_ge(experts_in, 16 * (3 + HC))
            pe.wait_ge(counts_ready, GROUPS)

            def transpose_block(a, n):
                pe.wait_ge(b_in[a % RING], 16 * (uses(a, n) + 1))
                wait(pe, b_xT, number(a, n) - 1)
                pe.transpose(ps_in(a), block_in[a % RING][:, 0:D], ident[:, :]).then_inc(b_x_psum, 1)

            def up(a, n, expert):
                t = number(a, n)
                pe.wait_ge(b_xT, t + 1)
                wait(pe, b_hidden, t - 1)
                pe.matmul(ps_up(a), block_T[a % 2], w1_sb[:, bass.ds(expert, 1), :].rearrange("p a h -> p (a h)"),
                          start=True, stop=True).then_inc(b_up, 1)

            def transpose_hidden(a, n):
                t = number(a, n)
                pe.wait_ge(b_hidden, t + 1)
                wait(pe, b_relu, t - 1)
                for c in range(HC):
                    last = pe.transpose(ps_hidden(a)[:, c * P:(c + 1) * P], hidden[a % 2][:, c * P:(c + 1) * P],
                                        ident[:, :])
                last.then_inc(b_t_psum, 1)

            def down(a, n, expert):
                t = number(a, n)
                pe.wait_ge(b_relu, t + 1)
                wait(pe, b_biased, t - 1)
                for c in range(HC):
                    last = pe.matmul(ps_down(a), hiddenT[a % 2][:, c * P:(c + 1) * P],
                                     w2_sb[:, bass.ds(expert, 1), c, :].rearrange("p a d -> p (a d)"),
                                     start=(c == 0), stop=(c == HC - 1))
                last.then_inc(b_down, 1)

            pe.wait_ge(experts_known, 16)

            def block_step(a, n, experts):
                transpose_block(a, n)
                if a > 1:
                    transpose_hidden(a - 2, n)
                if a > 2:
                    down(a - 3, n, experts[0])
                up(a, n, experts[3])

            blocks(pe, block_step, mybir.EngineType.PE)
            last = BLOCKS - 1
            experts = experts_from(mybir.EngineType.PE, last - 2, 3)
            transpose_hidden(last - 1, 0)
            down(last - 2, 0, experts[0])
            transpose_hidden(last, 0)
            down(last - 1, 0, experts[1])
            down(last, 0, experts[2])


_INS = ['L0_attn_x', 'L0_attn_Wq', 'L0_attn_Wk', 'L0_attn_Wv', 'L0_ffn_w_router', 'L0_ffn_b_router',
        'L0_ffn_w1', 'L0_ffn_b1', 'L0_ffn_w2', 'L0_ffn_b2']


def kernel(**inputs):
    import numpy as _np
    import concourse.bacc as _bacc
    from concourse import mybir as _mybir
    from concourse.bass_utils import run_bass_kernel_spmd as _run

    nc = _bacc.Bacc("TRN2", target_bir_lowering=False, num_devices=1)
    arrays, args = {}, []
    for name in _INS:
        a = _np.ascontiguousarray(inputs[name])
        arrays[f"in_{name}"] = a
        args.append(nc.dram_tensor(f"in_{name}", a.shape, _mybir.dt.from_np(a.dtype), kind="ExternalInput").ap())
    shape = inputs['L0_attn_x'].shape
    out = nc.dram_tensor("out", shape, _mybir.dt.from_np(_np.dtype("float32")), kind="ExternalOutput").ap()
    build_layer(nc, *args, out)
    r = _run(nc, [arrays], core_ids=[0])
    return r.results[0]["out"]
```

```python
from contextlib import ExitStack

import concourse.bass as bass
from concourse import mybir

F32 = mybir.dt.float32
F32R = mybir.dt.float32r
BF16 = mybir.dt.bfloat16
I32 = mybir.dt.int32
ACT = mybir.ActivationFunctionType
ALU = mybir.AluOpType
AX = mybir.AxisListType

P = 128
EPS = 1e-5
ROUTE_STEPS = 20
WARM_START, WARM_NORM, WARM_SPLIT, WARM_TABLE = 12, 18, 10, 56


def build_layer(nc, x, Wq, Wk, Wv, w_router, b_router, w1, b1, w2, b2, out):
    B, N, D = x.shape
    E, _, H = w1.shape
    T = 4
    G = T * P
    GROUPS = B * N // G
    PER_BATCH = N // G
    KC = N // P
    HC = H // P
    NORM = float(D) ** -0.5
    BLOCKS = (B * N - E) // P + E
    ROW = 2 * D + 4
    C_PROB, C_TOKEN, C_EXPERT = 2 * D, 2 * D + 1, 2 * D + 2
    NO_TOKEN = 1 << 20
    RING = 8
    BLOCKS_PEELED = 2 * RING - 1
    assert (BLOCKS - BLOCKS_PEELED) % RING == 0
    assert D == P and PER_BATCH == 2 and KC == 2 * T

    x_rows = x.rearrange("b n d -> (b n) d")
    x_tiles = x_rows.rearrange("(t p) d -> p t d", p=P)
    out_rows = out.rearrange("b n d -> (b n) d")
    table = nc.dram_tensor("expert_rows", (BLOCKS * P, ROW), F32, kind="Internal").ap()
    table_blocks = table.rearrange("(n p) c -> n p c", p=P)

    with ExitStack() as ctx:
        def sb(name, shape, dt=F32):
            return ctx.enter_context(nc.sbuf_tensor(name, shape, dt))

        def sem(name):
            return ctx.enter_context(nc.semaphore(name))

        x_all = sb("x_all", [P, GROUPS * T, D])
        keysT = sb("keysT", [P, 2, B * N], F32R)
        values = sb("values", [P, KC, D])
        probs = sb("probs", [P, 2 * T * N])
        qT = sb("qT", [P, 2, 2, G], F32R)
        probsT = sb("probsT", [P, 2, G])
        xn = sb("xn", [P, 2, T, D])
        mixedT = sb("mixedT", [P, 2, G])
        pay = sb("pay", [P, 2, T, ROW])
        pay_i = pay[:, :, :, :].bitcast(I32)
        xn2T = sb("xn2T", [P, G])
        w1_sb = sb("w1_sb", [P, E, H + HC])
        w2_sb = sb("w2_sb", [P, E, HC, D])
        b2_rep = sb("b2_rep", [P, E, D])
        wq_sb = sb("wq_sb", [P, D])
        wk_sb = sb("wk_sb", [P, D])
        wv_sb = sb("wv_sb", [P, D])
        wvT = sb("wvT", [P, D])
        m_hl = sb("m_hl", [P, 2, D], F32R)
        wr_sb = sb("wr_sb", [P, E])
        br_rep = sb("br_rep", [P, E])
        ident = sb("ident", [P, P])
        before_f = sb("before_f", [P, P])
        before = sb("before", [P, P], BF16)
        ones = sb("ones", [P, P], BF16)
        descend = sb("descend", [P, E])
        steps128 = sb("steps128", [P, T, E])
        tokens = sb("tokens", [P, GROUPS * T], I32)
        experts_of = sb("experts_of", [1, BLOCKS], I32)
        pad_rows = sb("pad_rows", [P, ROW])
        row_sum = sb("row_sum", [P, 2, T])
        weight = sb("weight", [P, 2, T])
        neg_max = sb("neg_max", [P, 2, T])
        stats1 = sb("stats1", [P, 2, T, 6])
        mv1 = sb("mv1", [P, 2, T, 2])
        rstd1 = sb("rstd1", [P, 2, T])
        shift1 = sb("shift1", [P, 2, T])
        stats2 = sb("stats2", [P, T, 6])
        mv2 = sb("mv2", [P, T, 2])
        minus_half = sb("minus_half", [P, T])
        rstd2 = sb("rstd2", [P, T])
        shift2 = sb("shift2", [P, T])
        logit = sb("logit", [P, T, E])
        logit_max = sb("logit_max", [P, T])
        below = sb("below", [P, T, E])
        rank_key = sb("rank_key", [P, T, E])
        best_key = sb("best_key", [P, T])
        exps = sb("exps", [P, T, E])
        exp_sum = sb("exp_sum", [P, T])
        chosen = sb("chosen", [P, 2, T, E])
        chosen_b = sb("chosen_b", [P, T, E], BF16)
        counts = sb("counts", [P, T + 1, E])
        cap = sb("cap", [P, E])
        nxt = sb("nxt", [P, E])
        need = sb("need", [P, E])
        over = sb("over", [P, T, E])
        scan = sb("scan", [P, 4, 2 * E])
        fresh = sb("fresh", [P, E])
        delta = sb("delta", [P, E])
        beyond = sb("beyond", [P, T, E])
        moved = sb("moved", [P, E])
        place = sb("place", [P, T, E])
        place1 = sb("place1", [P, T])
        position = sb("position", [P, 2, T], I32)

        def probs_tile(parity, j):
            at = (parity * T + j) * N
            return probs[:, at:at + N]

        at = [0]

        def carve(n):
            at[0] += n
            return probs[:, at[0] - n:at[0]]

        block_in = [carve(ROW) for _ in range(RING)]
        block_T = [carve(P) for _ in range(2)]
        block_token = [carve(1).bitcast(I32) for _ in range(RING)]
        block_w1 = [carve(H + HC) for _ in range(2)]
        hiddenT = [carve(H) for _ in range(2)]
        block_y = [carve(D) for _ in range(2)]
        block_out = [carve(D) for _ in range(RING)]

        ps_s = [ctx.enter_context(nc.psum_tensor(f"ps_s{n}", [P, N], F32)) for n in range(2)]
        ps_t = [ctx.enter_context(nc.psum_tensor(f"ps_t{n}", [P, G], F32)) for n in range(2)]
        ps_u = ctx.enter_context(nc.psum_tensor("ps_u", [P, G], F32))
        ps_m = ctx.enter_context(nc.psum_tensor("ps_m", [P, G], F32))

        x_in = [sem(f"x_in{n}") for n in range(3)]
        qk_in = sem("qk_in")
        v_in = sem("v_in")
        router_in = sem("router_in")
        experts_in = sem("experts_in")
        consts = sem("consts")
        half_ready = sem("half_ready")
        passed = sem("passed")
        pads_ready = sem("pads_ready")
        ident_ready = sem("ident_ready")
        m_psum = sem("m_psum")
        m_hi = sem("m_hi")
        m_lo = sem("m_lo")
        wvT_psum = sem("wvT_psum")
        wvT_ready = sem("wvT_ready")
        ln1 = sem("ln1")
        scale1 = sem("scale1")
        xn_ready = sem("xn_ready")
        xT_psum = sem("xT_psum")
        xT_hi = sem("xT_hi")
        xT_lo = sem("xT_lo")
        q_psum = sem("q_psum")
        q_hi = sem("q_hi")
        q_lo = sem("q_lo")
        values_in = [sem(f"values_in{n}") for n in range(2)]
        s_psum = sem("s_psum")
        max_ready = sem("max_ready")
        exp_ready = sem("exp_ready")
        weight_ready = sem("weight_ready")
        pT_psum = sem("pT_psum")
        pT_copied = [sem(f"pT_copied{n}") for n in range(2)]
        mixed = sem("mixed")
        mixedT_ready = sem("mixedT_ready")
        att_psum = sem("att_psum")
        x1_ready = sem("x1_ready")
        ln2 = sem("ln2")
        scale2 = sem("scale2")
        xn2_ready = sem("xn2_ready")
        xn2T_psum = sem("xn2T_psum")
        xn2T_ready = sem("xn2T_ready")
        logit_psum = sem("logit_psum")
        pick = sem("pick")
        exps_ready = sem("exps_ready")
        prob_ready = sem("prob_ready")
        chosen_ready = sem("chosen_ready")
        counts_psum = sem("counts_psum")
        counts_ready = sem("counts_ready")
        numbered = sem("numbered")
        route = sem("route")
        last_scatters = sem("last_scatters")
        rows_out = [sem(f"rows_out{n}") for n in range(2)]
        experts_known = sem("experts_known")
        b_in = [sem(f"b_in{n}") for n in range(RING)]
        b_x_psum = sem("b_x_psum")
        b_xT = sem("b_xT")
        b_token = sem("b_token")
        b_up = sem("b_up")
        b_w1 = sem("b_w1")
        b_relu = sem("b_relu")
        b_down = sem("b_down")
        b_biased = sem("b_biased")
        b_done = sem("b_done")
        b_out = [sem(f"b_out{n}") for n in range(RING)]

        def wait(eng, s, value):
            if not isinstance(value, int) or value > 0:
                eng.wait_ge(s, value)

        def apart(eng):
            eng.sem_inc(passed, 1)

        def parts(s, b):
            found = [2 * b + s + d for d in (0, -1, -2, 2, 1)]
            found = [v if not isinstance(v, int) or 0 <= v < GROUPS else None for v in found]
            return found

        def is_last_mix(g, p):
            return g is None and p is not None

        def ps_att(r):
            return ps_s[0] if is_last(r) else ps_m

        def is_first(g):
            return isinstance(g, int) and g == 0

        def is_last(r):
            return isinstance(r, int) and r == GROUPS - 1

        LAST = GROUPS + 2
        LOOP_FROM, LOOP_TO = 1, (GROUPS - 2) // 2

        def pipeline(eng, step):
            for i in range(2 * LOOP_FROM):
                step(i % 2, i // 2)
            with eng.Fori(LOOP_FROM, LOOP_TO) as b:
                for s in range(2):
                    step(s, b)
            for i in range(2 * LOOP_TO, LAST):
                step(i % 2, i // 2)

        LN1_STEPS = 2 * T
        LN2_STEPS = 2 * T
        POSITION_STEP = 16
        PICK_STEPS = 6
        CONSTS = 4 + E + T + 1 + 3 + 1

        ps_in = lambda a: (ps_u, ps_m)[a % 2][:, 0:P]
        ps_up = lambda a: ps_s[a % 2][:, 0:H]
        ps_down = lambda a: ps_t[a % 2][:, 0:D]

        def number(a, n):
            return a + RING * n

        def uses(a, n):
            return a // RING + n

        def experts_from(engine, at, count):
            cells = experts_of[0:1, bass.ds(at, count)]
            return nc.values_load_multi_w_load_instructions(
                cells, engines=[engine], min_val=0, max_val=E - 1,
                skip_runtime_bounds_check_because="each is an index among E experts, or a padding row's 0")[1]

        def blocks(eng, step, engine=None):
            def rounds(first, last, n):
                at = max(first - 3, 0)
                known = engine and experts_from(engine, number(at, n), last - at)
                for a in range(first, last):
                    step(a, n, known and [known[max(a - d, 0) - at] for d in (3, 2, 1, 0)])

            rounds(0, RING, 0)
            rounds(RING, BLOCKS_PEELED, 0)
            with eng.Fori(0, (BLOCKS - BLOCKS_PEELED) // RING) as n:
                rounds(BLOCKS_PEELED, BLOCKS_PEELED + RING, n)

        block = ctx.enter_context(nc.Block())

        @block.sync
        def _(sp):
            sp.dma_start(x_all[:, 0:T, :], x_tiles[:, 0:T, :]).then_inc(x_in[0], 16)
            sp.dma_start(wq_sb[:, :], Wq).then_inc(qk_in, 16)
            sp.dma_start(wk_sb[:, :], Wk).then_inc(qk_in, 16)
            sp.dma_start(x_all[:, T:2 * T, :], x_tiles[:, T:2 * T, :]).then_inc(x_in[1], 16)
            sp.dma_start(wv_sb[:, :], Wv).then_inc(v_in, 16)
            sp.dma_start(wr_sb[:, :], w_router).then_inc(router_in, 16)
            sp.dma_start(br_rep[:, :], b_router.partition_broadcast(P)).then_inc(router_in, 16)
            sp.dma_start(x_all[:, 2 * T:, :], x_tiles[:, 2 * T:, :]).then_inc(x_in[2], 16)

            def load_values(b):
                for h in range(2):
                    sp.wait_ge(xn_ready, T * (2 * b + h + 1))
                    apart(sp)
                    wait(sp, mixed, KC * (2 * b - 1) + T * h + T)
                    apart(sp)
                    sp.dma_start(values[:, T * h:T * h + T, :], xn[:, h, :, :]).then_inc(values_in[h], 16)

            load_values(0)
            sp.dma_start(w1_sb[:, :, 0:H], w1.rearrange("e d h -> d e h")).then_inc(experts_in, 16)
            for c in range(HC):
                sp.dma_start(w2_sb[:, :, c, :], w2[:, c * P:(c + 1) * P, :].rearrange("e p d -> p e d"))\
                  .then_inc(experts_in, 16)
            for c in range(HC):
                sp.dma_start(w1_sb[:, :, H + c:H + c + 1], b1[:, c * P:(c + 1) * P].rearrange("e p -> p e").unsqueeze(2),
                             allow_slow_non_contiguous=True).then_inc(experts_in, 16)
            sp.dma_start(b2_rep[:, :, :], b2.partition_broadcast(P)).then_inc(experts_in, 16)
            with sp.Fori(1, B) as b:
                load_values(b)

            for n in range(2):
                sp.wait_ge(rows_out[n], 16 + 16 * T * GROUPS // 2)
            sp.wait_ge(pT_psum, KC * GROUPS)

            first_rows = table_blocks[:, 0, C_EXPERT:C_EXPERT + 1].rearrange("n c -> c n")
            sp.dma_start(experts_of[0:1, :], first_rows.bitcast(I32),
                         allow_slow_non_contiguous=True).then_inc(experts_known, 16)

            def load_block(a, n, _):
                free = number(a, n) + 1 - RING
                wait(sp, b_done, free)
                apart(sp)
                wait(sp, b_token, free)
                apart(sp)
                rows = table_blocks[bass.ds(number(a, n), 1), :, :].rearrange("n p c -> p (n c)")
                sp.dma_start(block_in[a % RING], rows).then_inc(b_in[a % RING], 16)

            blocks(sp, load_block)
            for n in range(RING):
                sp.wait_ge(b_out[n], 16 * len(range(n, BLOCKS, RING)))

        @block.gpsimd
        def _(pool):
            pool.memset(ident[:, :], 0.0).then_inc(ident_ready, 1)
            pool.wait_ge(ident_ready, 1)
            pool.affine_select(out=ident[:, :], in_=ident[:, :], compare_op=ALU.not_equal, fill=1.0,
                               base=0, pattern=[[-1, P]], channel_multiplier=1).then_inc(ident_ready, 1)
            pool.memset(minus_half[:, :], -0.5).then_inc(half_ready, 1)
            pool.wait_ge(half_ready, 1)

            def rsqrt(mv, rstd, shift, step):
                count, base = step
                pool.tensor_scalar(rstd, mv[:, :, 1], EPS, None, ALU.add).then_inc(count, 1)
                pool.wait_ge(count, base + 1)
                pool.tensor_tensor(rstd, rstd, minus_half[:, :], ALU.pow).then_inc(count, 1)
                pool.wait_ge(count, base + 2)
                pool.tensor_tensor(shift, mv[:, :, 0], rstd, ALU.mult).then_inc(count, 1)
                pool.wait_ge(count, base + 3)
                apart(pool)
                pool.tensor_scalar(shift, shift, -1.0, None, ALU.mult).then_inc(count, 1)

            def scale_rows(k, s):
                pool.wait_ge(ln1, LN1_STEPS * k + LN1_STEPS)
                wait(pool, xn_ready, T * (k - 1))
                apart(pool)
                rsqrt(mv1[:, s, :, :], rstd1[:, s, :], shift1[:, s, :], (scale1, 4 * k))

            def scale_x1(r):
                pool.wait_ge(ln2, LN2_STEPS * r + LN2_STEPS)
                wait(pool, xn2_ready, T * r)
                apart(pool)
                rsqrt(mv2[:, :, :], rstd2[:, :], shift2[:, :], (scale2, 4 * r))

            for k in range(2):
                scale_rows(k, k)
            pool.memset(pad_rows[:, :], 0.0).then_inc(pads_ready, 1)
            pool.wait_ge(pads_ready, 1)
            pool.memset(pad_rows[:, C_TOKEN:C_TOKEN + 1].bitcast(I32), NO_TOKEN).then_inc(pads_ready, 1)
            pool.wait_ge(pads_ready, 2)
            table_columns = table.rearrange("(n p) c -> p n c", p=P)
            for n, (lo, hi) in enumerate(((0, BLOCKS // 2), (BLOCKS // 2, BLOCKS))):
                pool.dma_start(table_columns[:, lo:hi, :],
                             pad_rows[:, :].unsqueeze(1).to_broadcast([P, hi - lo, ROW])).then_inc(rows_out[n], 16)
            pool.memset(before_f[:, :], 1.0).then_inc(consts, 1)
            pool.wait_ge(consts, 1)
            pool.affine_select(out=before_f[:, :], in_=before_f[:, :], compare_op=ALU.is_gt, fill=0.0,
                               base=0, pattern=[[1, P]], channel_multiplier=-1).then_inc(consts, 1)
            pool.wait_ge(consts, 2)
            pool.tensor_copy(before[:, :], before_f[:, :]).then_inc(consts, 1)
            pool.memset(ones[:, :], 1.0).then_inc(consts, 1)
            for e in range(E):
                pool.memset(descend[:, e:e + 1], float(E - e)).then_inc(consts, 1)
            for j in range(T):
                pool.memset(steps128[:, j, :], float(P * j)).then_inc(consts, 1)
            pool.iota(tokens[:, :], pattern=[[P, GROUPS * T]], base=0, channel_multiplier=1).then_inc(consts, 1)
            for state in (cap, nxt, scan):
                pool.memset(state[:], 0.0).then_inc(consts, 1)
            pool.memset(pay[:, :, :, ROW - 1:ROW], 0.0).then_inc(consts, 1)
            pool.wait_ge(consts, CONSTS)

            def number_rows(r, s, b):
                wait(pool, rows_out[s], 16 + (b - 1) * 16 * T)
                apart(pool)
                pool.tensor_copy(pay_i[:, s, :, C_TOKEN], tokens[:, bass.ds(r * T, T)]).then_inc(numbered, 1)
                pool.wait_ge(pick, PICK_STEPS * r + 5)
                apart(pool)
                pool.tensor_scalar(pay_i[:, s, :, C_EXPERT], best_key[:, :], -1.0, float(E),
                                   ALU.mult, ALU.add).then_inc(numbered, 1)

            def scatter_rows(r, s):
                pool.wait_ge(route, ROUTE_STEPS * r + POSITION_STEP)
                apart(pool)
                pool.wait_ge(numbered, 2 * r + 2)
                pool.wait_ge(xn2_ready, T * r + T)
                pool.wait_ge(x1_ready, T * r + T)
                pool.wait_ge(prob_ready, 2 * r + 2)
                apart(pool)
                for j in range(T):
                    pool.indirect_dma_start(
                        out=table[:, :], out_offset=bass.IndirectOffsetOnAxis(ap=position[:, s, j:j + 1], axis=0),
                        in_=pay[:, s, j, :], in_offset=None,
                        bounds_check=BLOCKS * P - 1, oob_is_err=False).then_inc(rows_out[s], 16)
                    if is_last(r) and j == 2:
                        pool.sem_inc(last_scatters, 1)

            def step(s, b):
                g, p, r, k, u = parts(s, b)
                if r is not None:
                    scale_x1(r)
                if k is not None:
                    scale_rows(k, s)
                if is_last(r):
                    number_rows(r - 1, 1 - s, b)
                    scatter_rows(r - 1, 1 - s)
                if r is not None and not is_last_mix(g, p):
                    number_rows(r, s, b)
                    scatter_rows(r, s)
                if r is None and s == 1:
                    for n in range(2):
                        pool.wait_ge(rows_out[n], 16)

            pipeline(pool, step)

            def scatter_block(a, n, _):
                pool.wait_ge(b_done, number(a, n) + 1)
                apart(pool)
                pool.wait_ge(b_token, number(a, n) + 1)
                apart(pool)
                pool.indirect_dma_start(
                    out=out_rows, in_=block_out[a % RING], in_offset=None,
                    out_offset=bass.IndirectOffsetOnAxis(
                        ap=block_token[a % RING], axis=0),
                    bounds_check=B * N - 1, oob_is_err=False).then_inc(b_out[a % RING], 16)

            blocks(pool, scatter_block)

        @block.vector
        def _(dve):
            tt = dve.tensor_tensor

            def stats(src, bn, mv, count, base, part):
                if part in (0, None):
                    for j in range(T):
                        dve.bn_stats(out=bn[:, j, :], in_=src(j)).then_inc(count, 1)
                if part in (1, None):
                    for j in range(T):
                        dve.wait_ge(count, base + j + 1)
                        apart(dve)
                        dve.bn_aggr(out=mv[:, j, :], in_=bn[:, j, :]).then_inc(count, 1)

            def stats1_of(k, s, part=None):
                if part in (0, None):
                    if isinstance(k, int) and k < 2:
                        dve.wait_ge(x_in[k], 16)
                    else:
                        dve.wait_ge(x_in[2], 16)
                    wait(dve, scale1, 4 * (k - 1))
                stats(lambda j: x_all[:, bass.ds(k * T + j, 1), :].rearrange("p a d -> p (a d)"),
                      stats1[:, s, :, :], mv1[:, s, :, :], ln1, LN1_STEPS * k, part)

            def norm_rows(k, s):
                dve.wait_ge(scale1, 4 * k + 4)
                wait(dve, xT_psum, k - 1)
                wait(dve, values_in[s], 16 * (k // 2))
                for j in range(T):
                    dve.tensor_scalar(xn[:, s, j, :], x_all[:, k * T + j, :], rstd1[:, s, j:j + 1],
                                      shift1[:, s, j:j + 1], ALU.mult, ALU.add).then_inc(xn_ready, 1)

            def xT_lo_of(k, ps=ps_m):
                dve.wait_ge(xT_hi, k + 1)
                cols = bass.ds(k * G, G)
                tt(keysT[:, 1, cols], ps[:, :], keysT[:, 0, cols].bitcast(F32), ALU.subtract).then_inc(xT_lo, 1)

            def q_lo_of(k, s):
                dve.wait_ge(q_hi, k + 1)
                tt(qT[:, s, 1, :], ps_m[:, :], qT[:, s, 0, :].bitcast(F32), ALU.subtract).then_inc(q_lo, 1)

            stats1_of(0, 0)
            stats1_of(1, 1)
            dve.wait_ge(m_hi, 1)
            tt(m_hl[:, 1, :], ps_t[0][:, 0:D], m_hl[:, 0, :].bitcast(F32), ALU.subtract).then_inc(m_lo, 1)
            norm_rows(0, 0)
            xT_lo_of(0)
            q_lo_of(0, 0)
            xT_lo_of(1, ps_u)

            def step(s, b):
                g, p, r, k, u = parts(s, b)
                q = 1 - s

                def row_max(j):
                    if g is None:
                        return
                    dve.wait_ge(s_psum, T * g + j + 1)
                    wait(dve, exp_ready, T * (g - 2) + j + 1)
                    dve.tensor_reduce(out=neg_max[:, s, j:j + 1], in_=ps_s[j % 2][:, :], axis=AX.X,
                                      op=ALU.max, negate=True).then_inc(max_ready, 1)

                def evacuate(c):
                    if p is None:
                        return
                    dve.wait_ge(pT_psum, KC * p + c + 1)
                    wait(dve, mixed, KC * p + c - 1)
                    dve.tensor_copy(probsT[:, c % 2, :], ps_t[c % 2][:, :]).then_inc(pT_copied[c % 2], 1)

                def weights():
                    dve.wait_ge(exp_ready, T * p + T)
                    dve.reciprocal(weight[:, q, :], row_sum[:, q, :]).then_inc(weight_ready, 1)
                    dve.wait_ge(weight_ready, 2 * p + 1)
                    dve.tensor_scalar(weight[:, q, :], weight[:, q, :], NORM, None, ALU.mult)\
                       .then_inc(weight_ready, 1)

                def residual(j):
                    if j == 0:
                        dve.wait_ge(att_psum, r + 1)
                        dve.wait_ge(weight_ready, 2 * r + 2)
                        wait(dve, rows_out[s], 16 + (b - 1) * 16 * T)
                    dve.scalar_tensor_tensor(
                        pay[:, s, j, D:2 * D], ps_att(r)[:, j * D:(j + 1) * D], weight[:, s, j:j + 1],
                        x_all[:, bass.ds(r * T + j, 1), :].rearrange("p a d -> p (a d)"),
                        ALU.mult, ALU.add).then_inc(x1_ready, 1)

                def stats2_of(part):
                    if part == 0:
                        dve.wait_ge(x1_ready, T * r + T)
                        wait(dve, scale2, 4 * r)
                    stats(lambda j: pay[:, s, j, D:2 * D], stats2, mv2, ln2, LN2_STEPS * r, part)

                def choose(r, s):
                    per_expert = lambda v: v.unsqueeze(2).to_broadcast([P, T, E])
                    over_tiles = lambda v: v.unsqueeze(1).to_broadcast([P, T, E])
                    dve.wait_ge(logit_psum, r + 1)
                    tt(logit[:, :, :], ps_m[:, 0:T * E].rearrange("p (t e) -> p t e", e=E),
                       over_tiles(br_rep[:, :]), ALU.add).then_inc(pick, 1)
                    dve.wait_ge(pick, PICK_STEPS * r + 1)
                    dve.tensor_reduce(out=logit_max[:, :], in_=logit[:, :, :], axis=AX.X,
                                      op=ALU.max).then_inc(pick, 1)
                    dve.wait_ge(pick, PICK_STEPS * r + 2)
                    wait(dve, exps_ready, r)
                    tt(below[:, :, :], logit[:, :, :], per_expert(logit_max[:, :]), ALU.subtract)\
                        .then_inc(pick, 1)
                    dve.wait_ge(pick, PICK_STEPS * r + 3)
                    wait(dve, numbered, 2 * r)
                    dve.scalar_tensor_tensor(rank_key[:, :, :], below[:, :, :], 0.0, over_tiles(descend[:, :]),
                                             ALU.is_ge, ALU.mult).then_inc(pick, 1)
                    dve.wait_ge(pick, PICK_STEPS * r + 4)
                    dve.tensor_reduce(out=best_key[:, :], in_=rank_key[:, :, :], axis=AX.X,
                                      op=ALU.max).then_inc(pick, 1)
                    dve.wait_ge(pick, PICK_STEPS * r + 5)
                    wait(dve, counts_psum, r)
                    tt(chosen_b[:, :, :], rank_key[:, :, :], per_expert(best_key[:, :]), ALU.is_equal)\
                        .then_inc(chosen_ready, 1)
                    tt(chosen[:, s, :, :], rank_key[:, :, :], per_expert(best_key[:, :]), ALU.is_equal)\
                        .then_inc(pick, 1)

                def place_rows(r, s, part):
                    last = [0 if part == 0 else 9]

                    def did(ins):
                        ins.then_inc(route, 1)
                        last[0] += 1

                    def after(n):
                        dve.wait_ge(route, ROUTE_STEPS * r + n)

                    over_tiles = lambda v: v.unsqueeze(1).to_broadcast([P, T, E])
                    total = counts[:, T, :]
                    ranks = counts[:, 0:T, :]
                    if part == 0:
                        dve.wait_ge(counts_ready, r + 1)
                        wait(dve, route, ROUTE_STEPS * r)
                        did(tt(need[:, :], total, cap[:, :], ALU.subtract))
                        did(tt(beyond[:, :, :], ranks, over_tiles(cap[:, :]), ALU.is_ge))
                        did(tt(place[:, :, :], ranks, over_tiles(nxt[:, :]), ALU.add))
                        after(1)
                        did(tt(over[:, :, :], over_tiles(need[:, :]), steps128[:, :, :], ALU.is_gt))
                        after(4)
                        did(dve.reduce_sum(scan[:, 0, E:2 * E], over[:, :, :].rearrange("p t e -> p e t"),
                                           axis=AX.X))
                        for n in range(3):
                            after(5 + n)
                            did(tt(scan[:, n + 1, E - 1:2 * E], scan[:, n, E - 1:2 * E],
                                   scan[:, n, E - 1 - (1 << n):2 * E - (1 << n)], ALU.add))
                        after(8)
                        did(dve.scalar_tensor_tensor(fresh[:, :], scan[:, 3, E - 1:2 * E - 1], float(P), cap[:, :],
                                                     ALU.mult, ALU.subtract))
                        return
                    after(9)
                    did(tt(delta[:, :], fresh[:, :], nxt[:, :], ALU.subtract))
                    after(10)
                    did(tt(beyond[:, :, :], beyond[:, :, :], over_tiles(delta[:, :]), ALU.mult))
                    after(11)
                    did(tt(place[:, :, :], place[:, :, :], beyond[:, :, :], ALU.add))
                    after(12)
                    dve.wait_ge(pick, PICK_STEPS * r + 6)
                    did(tt(place[:, :, :], place[:, :, :], chosen[:, s, :, :], ALU.mult))
                    after(13)
                    did(dve.reduce_sum(place1[:, :], place[:, :, :], axis=AX.X))
                    did(tt(nxt[:, :], nxt[:, :], total, ALU.add))
                    after(14)
                    did(dve.tensor_copy(position[:, s, :], place1[:, :]))
                    assert last[0] == POSITION_STEP
                    did(tt(moved[:, :], over[:, 0, :], delta[:, :], ALU.mult))
                    did(dve.scalar_tensor_tensor(cap[:, :], scan[:, 0, E:2 * E], float(P), need[:, :],
                                                 ALU.mult, ALU.subtract))
                    after(17)
                    did(tt(nxt[:, :], nxt[:, :], moved[:, :], ALU.add))
                    did(tt(scan[:, 0, E - 1:E], scan[:, 0, E - 1:E], scan[:, 3, 2 * E - 1:2 * E],
                           ALU.add))
                    assert last[0] == ROUTE_STEPS

                def probability(r, s):
                    dve.wait_ge(exps_ready, r + 1)
                    dve.reduce_sum(exp_sum[:, :], exps[:, :, :], axis=AX.X).then_inc(prob_ready, 1)
                    dve.wait_ge(prob_ready, 2 * r + 1)
                    dve.reciprocal(pay[:, s, :, C_PROB], exp_sum[:, :]).then_inc(prob_ready, 1)

                if is_first(g):
                    stats1_of(k, s)
                    row_max(0)
                    row_max(1)
                    q_lo_of(u, q)
                    norm_rows(k, s)
                    row_max(2)
                    row_max(3)
                    xT_lo_of(k)
                    dve.wait_ge(router_in, 32)
                    dve.wait_ge(consts, CONSTS)
                    return
                row_max(0)
                if p is not None:
                    weights()
                if r is not None:
                    for j in range(T):
                        residual(j)
                    stats2_of(0)
                    stats2_of(1)
                row_max(1)
                if k is not None:
                    stats1_of(k, s)
                if u is not None:
                    q_lo_of(u, q)
                row_max(2)
                evacuate(6)
                if is_last(r):
                    choose(r - 1, q)
                    place_rows(r - 1, q, 0)
                    place_rows(r - 1, q, 1)
                    probability(r - 1, q)
                if r is not None and not is_last_mix(g, p):
                    choose(r, s)
                row_max(3)
                if r is not None and not is_last_mix(g, p):
                    probability(r, s)
                    place_rows(r, s, 0)
                if k is not None:
                    xT_lo_of(k)
                if r is not None and not is_last_mix(g, p):
                    place_rows(r, s, 1)

            pipeline(dve, step)

            dve.wait_ge(experts_in, 16 * (2 + 2 * HC))

            def weights_of(a, n, expert):
                wait(dve, b_relu, number(a, n) - 1)
                dve.tensor_copy(block_w1[a % 2], w1_sb[:, bass.ds(expert, 1), :].rearrange("p a h -> p (a h)"))\
                   .then_inc(b_w1, 1)

            def output_of(a, n, expert):
                t = number(a, n)
                rows = block_in[a % RING]
                dve.wait_ge(b_down, t + 1)
                dve.wait_ge(b_in[a % RING], 16 * (uses(a, n) + 1))
                tt(block_y[a % 2], ps_down(a), b2_rep[:, bass.ds(expert, 1), :].rearrange("p a d -> p (a d)"),
                   ALU.add).then_inc(b_biased, 1)
                dve.wait_ge(b_biased, t + 1)
                wait(dve, b_out[a % RING], 16 * uses(a, n))
                dve.scalar_tensor_tensor(block_out[a % RING], block_y[a % 2], rows[:, C_PROB:C_PROB + 1],
                                         rows[:, D:2 * D], ALU.mult, ALU.add).then_inc(b_done, 1)

            dve.wait_ge(experts_known, 16)

            def block_step(a, n, experts):
                weights_of(a, n, experts[3])
                if a > 2:
                    output_of(a - 3, n, experts[0])

            blocks(dve, block_step, mybir.EngineType.DVE)
            experts = experts_from(mybir.EngineType.DVE, BLOCKS - 3, 3)
            for d in range(3):
                output_of(BLOCKS - 3 + d, 0, experts[d])

        @block.scalar
        def _(act):
            ln_apply = lambda dst, src, rstd, shift: act.activation(dst, src, ACT.Identity, bias=shift, scale=rstd)

            def norm1(k, s, batch):
                act.wait_ge(scale1, 4 * k + 4)
                wait(act, xT_psum, k - 1)
                wait(act, values_in[s], 16 * batch)
                for j in range(T):
                    ln_apply(xn[:, s, j, :], x_all[:, bass.ds(k * T + j, 1), :].rearrange("p a d -> p (a d)"),
                             rstd1[:, s, j:j + 1], shift1[:, s, j:j + 1]).then_inc(xn_ready, 1)

            def xT_hi_of(k, ps=ps_m):
                act.wait_ge(xT_psum, k + 1)
                act.copy(keysT[:, 0, bass.ds(k * G, G)], ps[:, :]).then_inc(xT_hi, 1)

            def q_hi_of(k, s):
                act.wait_ge(q_psum, k + 1)
                wait(act, s_psum, T * (k - 2) + T)
                act.copy(qT[:, s, 0, :], ps_m[:, :]).then_inc(q_hi, 1)

            act.wait_ge(m_psum, 1)
            act.copy(m_hl[:, 0, :], ps_t[0][:, 0:D]).then_inc(m_hi, 1)
            xT_hi_of(0)
            norm1(1, 1, 0)
            q_hi_of(0, 0)
            xT_hi_of(1, ps_u)

            def step(s, b):
                g, p, r, k, u = parts(s, b)
                q = 1 - s

                def exponentials(j):
                    if g is None:
                        return
                    act.wait_ge(max_ready, T * g + j + 1)
                    if j == 0:
                        wait(act, pT_psum, KC * (g - 2) + KC)
                        wait(act, weight_ready, 2 * (g - 2) + 2)
                    act.activation(probs_tile(s, j), ps_s[j % 2][:, :], ACT.Exp, bias=neg_max[:, s, j:j + 1],
                                   accum_out=row_sum[:, s, j:j + 1]).then_inc(exp_ready, 1)

                def evacuate(c):
                    if p is None:
                        return
                    act.wait_ge(pT_psum, KC * p + c + 1)
                    wait(act, mixed, KC * p + c - 1)
                    act.copy(probsT[:, c % 2, :], ps_t[c % 2][:, :]).then_inc(pT_copied[c % 2], 1)

                def norm2():
                    act.wait_ge(scale2, 4 * r + 4)
                    wait(act, rows_out[s], 16 + (b - 1) * 16 * T)
                    for j in range(T):
                        ln_apply(pay[:, s, j, 0:D], pay[:, s, j, D:2 * D], rstd2[:, j:j + 1],
                                 shift2[:, j:j + 1]).then_inc(xn2_ready, 1)

                def mixed_out(v, parity):
                    act.wait_ge(mixed, KC * v + KC)
                    wait(act, att_psum, v)
                    act.copy(mixedT[:, parity, :], ps_u[:, :]).then_inc(mixedT_ready, 1)

                def small_copies(r):
                    act.wait_ge(pick, PICK_STEPS * r + 3)
                    wait(act, prob_ready, 2 * r)
                    act.activation(exps[:, :, :], below[:, :, :], ACT.Exp).then_inc(exps_ready, 1)
                    act.wait_ge(counts_psum, r + 1)
                    wait(act, route, ROUTE_STEPS * r)
                    act.copy(counts[:, :, :], ps_m[:, 0:(T + 1) * E].rearrange("p (t e) -> p t e", e=E))\
                       .then_inc(counts_ready, 1)

                if r is not None and not is_last(r):
                    mixed_out(r, s)
                if is_first(g):
                    act.wait_ge(wvT_psum, 1)
                    act.copy(wvT[:, :], ps_t[1][:, 0:D]).then_inc(wvT_ready, 1)
                    exponentials(0)
                    q_hi_of(u, q)
                    exponentials(1)
                    exponentials(2)
                    exponentials(3)
                    xT_hi_of(k)
                    return
                evacuate(0)
                evacuate(1)
                exponentials(0)
                evacuate(2)
                evacuate(3)
                evacuate(4)
                exponentials(1)
                if u is not None:
                    q_hi_of(u, q)
                if g is None:
                    evacuate(5)
                    evacuate(7)
                if r is not None:
                    norm2()
                if is_last(r):
                    small_copies(r - 1)
                if g is not None:
                    evacuate(5)
                elif p is not None:
                    mixed_out(p, q)
                if r is not None:
                    act.wait_ge(xn2T_psum, r + 1)
                    wait(act, logit_psum, r)
                    act.copy(xn2T[:, :], ps_m[:, :]).then_inc(xn2T_ready, 1)
                exponentials(2)
                if k is not None:
                    norm1(k, s, b + 1)
                if g is not None:
                    evacuate(7)
                if r is not None and not is_last_mix(g, p):
                    small_copies(r)
                exponentials(3)
                if k is not None:
                    xT_hi_of(k)

            pipeline(act, step)

            def transposed(a, n):
                t = number(a, n)
                act.wait_ge(b_x_psum, t + 1)
                wait(act, b_up, t - 1)
                act.copy(block_T[a % 2], ps_in(a)).then_inc(b_xT, 1)

            def tokens_of(a, n):
                act.wait_ge(b_in[a % RING], 16 * (uses(a, n) + 1))
                wait(act, b_out[a % RING], 16 * uses(a, n))
                apart(act)
                act.copy(block_token[a % RING], block_in[a % RING][:, C_TOKEN:C_TOKEN + 1].bitcast(I32))\
                   .then_inc(b_token, 1)

            def relu(a, n):
                t = number(a, n)
                act.wait_ge(b_up, t + 1)
                wait(act, b_down, t - 1)
                for c in range(HC):
                    last = act.activation(hiddenT[a % 2][:, c * P:(c + 1) * P], ps_up(a)[:, c * P:(c + 1) * P],
                                          ACT.Relu, bias=block_w1[a % 2][:, H + c:H + c + 1])
                last.then_inc(b_relu, 1)

            def block_step(a, n, _):
                transposed(a, n)
                if a > 0:
                    relu(a - 1, n)
                tokens_of(a, n)

            blocks(act, block_step)
            relu(BLOCKS - 1, 0)

        @block.tensor
        def _(pe):
            HI_LO = ((0, 0), (0, 1), (1, 0))

            def transpose_rows(k, s, ps=ps_m):
                pe.wait_ge(xn_ready, T * k + T)
                for j in range(T):
                    last = pe.transpose(ps[:, j * P:(j + 1) * P], xn[:, s, j, :], ident[:, :])
                last.then_inc(xT_psum, 1)

            def queries(k):
                pe.wait_ge(xT_lo, k + 1)
                for n, (wh, xh) in enumerate(HI_LO):
                    last = pe.matmul(ps_m[:, :], m_hl[:, wh, :], keysT[:, xh, bass.ds(k * G, G)],
                                     start=(n == 0), stop=(n == 2))
                last.then_inc(q_psum, 1)

            def keep_warm(count, bank=ps_s[1]):
                for _ in range(count):
                    pe.transpose(bank[:, 0:P], ident[:, :], ident[:, :])

            pe.wait_ge(ident_ready, 2)
            keep_warm(WARM_START)
            pe.wait_ge(qk_in, 32)
            pe.matmul(ps_t[0][:, 0:D], wq_sb[:, :], wk_sb[:, :], start=True, stop=True).then_inc(m_psum, 1)
            pe.wait_ge(v_in, 16)
            pe.transpose(ps_t[1][:, 0:D], wv_sb[:, :], ident[:, :]).then_inc(wvT_psum, 1)
            keep_warm(WARM_NORM)
            transpose_rows(0, 0)
            keep_warm(WARM_SPLIT)
            pe.wait_ge(m_lo, 1)
            queries(0)
            transpose_rows(1, 1, ps_u)
            keep_warm(WARM_SPLIT)

            def step(s, b):
                g, p, r, k, u = parts(s, b)
                q = 1 - s

                def logits(j):
                    if g is None:
                        return
                    if j == 0:
                        pe.wait_ge(q_lo, g + 1)
                        pe.wait_ge(xT_lo, PER_BATCH * (b + 1))
                    wait(pe, exp_ready, T * g + j - 1)
                    for n, (qh, kh) in enumerate(HI_LO):
                        for h in range(N // G):
                            last = pe.matmul(ps_s[j % 2][:, h * G:(h + 1) * G], qT[:, s, qh, j * P:(j + 1) * P],
                                             keysT[:, kh, bass.ds(b * N + h * G, G)],
                                             start=(n == 0), stop=(n == 2))
                    last.then_inc(s_psum, 1)

                def transposes(c):
                    if p is None:
                        return
                    if c == 0:
                        pe.wait_ge(exp_ready, T * p + T)
                    wait(pe, pT_copied[c % 2], T * p + c // 2)
                    for j in range(T):
                        last = pe.transpose(ps_t[c % 2][:, j * P:(j + 1) * P],
                                            probs_tile(q, j)[:, c * P:(c + 1) * P], ident[:, :])
                    last.then_inc(pT_psum, 1)

                def mix(c):
                    if p is None:
                        return
                    if c % T == 0:
                        pe.wait_ge(values_in[c // T], 16 * (b + 1 - q))
                    if c == 0:
                        wait(pe, mixedT_ready, p)
                    pe.wait_ge(pT_copied[c % 2], T * p + c // 2 + 1)
                    pe.matmul(ps_u[:, :], values[:, c, :], probsT[:, c % 2, :],
                              start=(c == 0), stop=(c == KC - 1)).then_inc(mixed, 1)

                def attend(v, parity):
                    pe.wait_ge(mixedT_ready, v + 1)
                    if is_last(v):
                        pe.wait_ge(exp_ready, T * GROUPS)
                    else:
                        wait(pe, counts_ready, v)
                        pe.wait_ge(xT_lo, k if k is not None else GROUPS)
                    for j in range(T):
                        last = pe.matmul(ps_att(v)[:, j * D:(j + 1) * D],
                                         mixedT[:, parity, j * P:(j + 1) * P], wvT[:, :],
                                         start=True, stop=True)
                    last.then_inc(att_psum, 1)

                def transpose_xn2():
                    pe.wait_ge(xn2_ready, T * r + T)
                    pe.wait_ge(x1_ready, T * r + T)
                    if is_last(r):
                        pe.wait_ge(counts_ready, r)
                    pe.wait_ge(q_lo, GROUPS if u is None else u + 1)
                    for j in range(T):
                        last = pe.transpose(ps_m[:, j * P:(j + 1) * P], pay[:, s, j, 0:D], ident[:, :])
                    last.then_inc(xn2T_psum, 1)

                def router():
                    pe.wait_ge(xn2T_ready, r + 1)
                    for j in range(T):
                        last = pe.matmul(ps_m[:, j * E:(j + 1) * E], xn2T[:, j * P:(j + 1) * P], wr_sb[:, :],
                                         start=True, stop=True)
                    last.then_inc(logit_psum, 1)

                def count():
                    pe.wait_ge(pick, PICK_STEPS * r + 1)
                    pe.wait_ge(chosen_ready, r + 1)
                    for j in range(T + 1):
                        out_j = ps_m[:, j * E:(j + 1) * E]
                        for i in range(min(j, T)):
                            last = pe.matmul(out_j, ones[:, :], chosen_b[:, i, :], start=(i == 0),
                                             stop=(j == T and i == T - 1))
                        if j < T:
                            last = pe.matmul(out_j, before[:, :], chosen_b[:, j, :], start=(j == 0), stop=True)
                    last.then_inc(counts_psum, 1)

                if is_first(g):
                    logits(0)
                    logits(1)
                    queries(u)
                    logits(2)
                    logits(3)
                    pe.wait_ge(q_lo, u + 1)
                    transpose_rows(k, s)
                    keep_warm(WARM_SPLIT, ps_u)
                    pe.wait_ge(wvT_ready, 1)
                    pe.wait_ge(router_in, 32)
                    pe.wait_ge(consts, CONSTS)
                    return
                if r is None:
                    logits(0)
                transposes(0)
                transposes(1)
                if r is not None:
                    logits(0)
                mix(0)
                if r is not None and not is_last(r):
                    attend(r, s)
                transposes(2)
                mix(1)
                logits(1)
                transposes(3)
                mix(2)
                transposes(4)
                mix(3)
                if u is not None:
                    if r is not None:
                        pe.wait_ge(x1_ready, T * r + T)
                    queries(u)
                logits(2)
                transposes(5)
                mix(4)
                if is_last_mix(g, p):
                    transposes(6)
                    mix(5)
                    transposes(7)
                    mix(6)
                    mix(7)
                    transpose_xn2()
                    attend(p, q)
                    router()
                    count()
                    return
                if r is not None:
                    transpose_xn2()
                transposes(6)
                mix(5)
                if r is not None:
                    router()
                logits(3)
                transposes(7)
                if r is not None:
                    count()
                mix(6)
                if k is not None:
                    if r is not None:
                        pe.wait_ge(counts_ready, r + 1)
                    pe.wait_ge(q_lo, u + 1)
                    transpose_rows(k, s)
                mix(7)

            pipeline(pe, step)

            pe.wait_ge(experts_in, 16 * (2 + 2 * HC))
            pe.wait_ge(counts_ready, GROUPS)

            def transpose_block(a, n):
                pe.wait_ge(b_in[a % RING], 16 * (uses(a, n) + 1))
                wait(pe, b_xT, number(a, n) - 1)
                pe.transpose(ps_in(a), block_in[a % RING][:, 0:D], ident[:, :]).then_inc(b_x_psum, 1)

            def up(a, n):
                t = number(a, n)
                pe.wait_ge(b_xT, t + 1)
                pe.wait_ge(b_w1, t + 1)
                wait(pe, b_relu, t - 1)
                for c in range(HC):
                    last = pe.matmul(ps_up(a)[:, c * P:(c + 1) * P], block_w1[a % 2][:, c * P:(c + 1) * P],
                                     block_T[a % 2], start=True, stop=True)
                last.then_inc(b_up, 1)

            def down(a, n, expert):
                t = number(a, n)
                pe.wait_ge(b_relu, t + 1)
                wait(pe, b_biased, t - 1)
                for c in range(HC):
                    last = pe.matmul(ps_down(a), hiddenT[a % 2][:, c * P:(c + 1) * P],
                                     w2_sb[:, bass.ds(expert, 1), c, :].rearrange("p a d -> p (a d)"),
                                     start=(c == 0), stop=(c == HC - 1))
                last.then_inc(b_down, 1)

            pe.wait_ge(last_scatters, 1)
            keep_warm(WARM_TABLE)
            pe.wait_ge(experts_known, 16)

            def block_step(a, n, experts):
                transpose_block(a, n)
                if a > 0:
                    up(a - 1, n)
                if a > 1:
                    down(a - 2, n, experts[1])

            blocks(pe, block_step, mybir.EngineType.PE)
            last = BLOCKS - 1
            experts = experts_from(mybir.EngineType.PE, last - 1, 2)
            up(last, 0)
            down(last - 1, 0, experts[0])
            down(last, 0, experts[1])


_INS = ['L0_attn_x', 'L0_attn_Wq', 'L0_attn_Wk', 'L0_attn_Wv', 'L0_ffn_w_router', 'L0_ffn_b_router',
        'L0_ffn_w1', 'L0_ffn_b1', 'L0_ffn_w2', 'L0_ffn_b2']


def kernel(**inputs):
    import numpy as _np
    import concourse.bacc as _bacc
    from concourse import mybir as _mybir
    from concourse.bass_utils import run_bass_kernel_spmd as _run

    nc = _bacc.Bacc("TRN2", target_bir_lowering=False, num_devices=1)
    arrays, args = {}, []
    for name in _INS:
        a = _np.ascontiguousarray(inputs[name])
        arrays[f"in_{name}"] = a
        args.append(nc.dram_tensor(f"in_{name}", a.shape, _mybir.dt.from_np(a.dtype), kind="ExternalInput").ap())
    shape = inputs['L0_attn_x'].shape
    out = nc.dram_tensor("out", shape, _mybir.dt.from_np(_np.dtype("float32")), kind="ExternalOutput").ap()
    build_layer(nc, *args, out)
    r = _run(nc, [arrays], core_ids=[0])
    return r.results[0]["out"]
```
